# Optimizing a Trainium2 kernel written in Bass

```python
import numpy as np
import jax
import jax.numpy as jnp

def _softmax(x, axis=-1):
    return jax.nn.softmax(x, axis=axis)

def _gelu(x):
    return jax.nn.gelu(x, approximate=True)

def _silu(x):
    return jax.nn.silu(x)

def _sigmoid(x):
    return jax.nn.sigmoid(x)

def _layernorm(x, axis=-1, eps=1e-05):
    m = jnp.mean(x, axis=axis, keepdims=True)
    v = jnp.var(x, axis=axis, keepdims=True)
    return (x - m) / jnp.sqrt(v + eps)

def _scatter_add(tgt, idx, src, axis=0):
    return tgt.at[idx].add(src)

def _segment_sum(src, seg, n):
    return jax.ops.segment_sum(src, seg, n)
kernel_name = 'mk_hybrid_d1_jaxref_r8_984778'

def setup_inputs(seed: int=0):
    np.random.seed(seed)
    _w = jnp.asarray

    def _L0_attn_a_setup():
        import jax, jax.numpy as jnp
        import numpy as np
        HEADS = 16
        HEAD_DIM = 64
        DIM = 128
        INNER = HEADS * HEAD_DIM

        def rotate_half(t):
            x1, x2 = jnp.split(t, 2, axis=-1)
            return jnp.concatenate((-x2, x1), axis=-1)

        def rope_table(n, head_dim, dtype):
            inv_freq = 1.0 / 10000.0 ** (jnp.arange(0, head_dim, 2, dtype=jnp.float32) / head_dim)
            freqs = jnp.arange(n, dtype=jnp.float32)[:, None] * inv_freq[None, :]
            return jnp.concatenate((freqs, freqs), axis=-1).astype(dtype)
        key = jax.random.key(seed)
        k1, k2, k3, k4 = jax.random.split(key, 4)
        x = jax.random.normal(k1, (1, 512, DIM), dtype=jnp.float32)
        s = 0.02
        W_qkv = jax.random.normal(k2, (DIM, 3 * INNER), dtype=jnp.float32) * s
        W_o1 = jax.random.normal(k3, (INNER, DIM), dtype=jnp.float32) * s
        W_o2 = jax.random.normal(k4, (DIM, DIM), dtype=jnp.float32) * s
        gamma = jnp.ones((DIM,), dtype=jnp.float32)
        return {'x': x, 'W_qkv': W_qkv, 'W_o1': W_o1, 'W_o2': W_o2, 'gamma': gamma}
    _L0_attn_a_in = _L0_attn_a_setup()

    def _L0_attn_b_setup():
        import jax, jax.numpy as jnp
        import numpy as np
        from math import sqrt
        D_MODEL = 128
        B, T = (4, 512)
        key = jax.random.key(seed)
        kx, kqk, kvo = jax.random.split(key, 3)
        x = jax.random.normal(kx, (B, T, D_MODEL), dtype=jnp.float32)
        limit = sqrt(6.0 / (2 * D_MODEL))
        QK = jax.random.uniform(kqk, (D_MODEL, D_MODEL), minval=-limit, maxval=limit, dtype=jnp.float32)
        VO = jax.random.uniform(kvo, (D_MODEL, D_MODEL), minval=-limit, maxval=limit, dtype=jnp.float32)
        return {'x': x, 'QK': QK, 'VO': VO}
    _L0_attn_b_in = _L0_attn_b_setup()

    def _L0_ffn_setup():
        import jax, jax.numpy as jnp
        import numpy as np
        B, S, D, H, E = (4, 256, 128, 512, 8)
        THRESHOLD = 0.5
        key = jax.random.key(seed)
        ks = jax.random.split(key, 7)
        s_in = 1.0 / np.sqrt(D)
        s_h = 1.0 / np.sqrt(H)
        return {'x': jax.random.normal(ks[0], (B, S, D), dtype=jnp.float32), 'Wg': jax.random.uniform(ks[1], (D, E), jnp.float32, -s_in, s_in), 'bg': jax.random.uniform(ks[2], (E,), jnp.float32, -s_in, s_in), 'W1': jax.random.uniform(ks[3], (E, D, H), jnp.float32, -s_in, s_in), 'b1': jax.random.uniform(ks[4], (E, H), jnp.float32, -s_in, s_in), 'W2': jax.random.uniform(ks[5], (E, H, D), jnp.float32, -s_h, s_h), 'b2': jax.random.uniform(ks[6], (E, D), jnp.float32, -s_h, s_h)}
    _L0_ffn_in = _L0_ffn_setup()
    _d = {'L0_attn_a_x': _L0_attn_a_in['x'], 'L0_attn_a_W_qkv': _L0_attn_a_in['W_qkv'], 'L0_attn_a_W_o1': _L0_attn_a_in['W_o1'], 'L0_attn_a_W_o2': _L0_attn_a_in['W_o2'], 'L0_attn_a_gamma': _L0_attn_a_in['gamma'], 'L0_attn_b_QK': _L0_attn_b_in['QK'], 'L0_attn_b_VO': _L0_attn_b_in['VO'], 'L0_ffn_Wg': _L0_ffn_in['Wg'], 'L0_ffn_bg': _L0_ffn_in['bg'], 'L0_ffn_W1': _L0_ffn_in['W1'], 'L0_ffn_b1': _L0_ffn_in['b1'], 'L0_ffn_W2': _L0_ffn_in['W2'], 'L0_ffn_b2': _L0_ffn_in['b2']}
    _x0 = _d['L0_attn_a_x']
    _d['L0_attn_a_x'] = jax.random.normal(jax.random.fold_in(jax.random.key(seed), 1), (2, 1024, 128), dtype=_x0.dtype)
    del _x0
    return _d

def reference(L0_attn_a_x, L0_attn_a_W_qkv, L0_attn_a_W_o1, L0_attn_a_W_o2, L0_attn_a_gamma, L0_attn_b_QK, L0_attn_b_VO, L0_ffn_Wg, L0_ffn_bg, L0_ffn_W1, L0_ffn_b1, L0_ffn_W2, L0_ffn_b2):

    def _L0_attn_a_ref(x, W_qkv, W_o1, W_o2, gamma):
        import jax, jax.numpy as jnp
        import numpy as np
        HEADS = 16
        HEAD_DIM = 64
        DIM = 128
        INNER = HEADS * HEAD_DIM

        def rotate_half(t):
            x1, x2 = jnp.split(t, 2, axis=-1)
            return jnp.concatenate((-x2, x1), axis=-1)

        def rope_table(n, head_dim, dtype):
            inv_freq = 1.0 / 10000.0 ** (jnp.arange(0, head_dim, 2, dtype=jnp.float32) / head_dim)
            freqs = jnp.arange(n, dtype=jnp.float32)[:, None] * inv_freq[None, :]
            return jnp.concatenate((freqs, freqs), axis=-1).astype(dtype)
        b, n, _ = x.shape
        scale = HEAD_DIM ** (-0.5)
        qkv = x @ W_qkv
        q, k, v = jnp.split(qkv, 3, axis=-1)
        to_heads = lambda t: t.reshape(b, n, HEADS, HEAD_DIM).transpose(0, 2, 1, 3)
        q, k, v = (to_heads(q), to_heads(k), to_heads(v))
        pos = rope_table(n, HEAD_DIM, x.dtype)
        cos, sin = (jnp.cos(pos), jnp.sin(pos))
        apply_rope = lambda t: t * cos + rotate_half(t) * sin
        q, k = (apply_rope(q), apply_rope(k))
        dots = jnp.einsum('bhid,bhjd->bhij', q, k) * scale
        causal = jnp.triu(jnp.ones((n, n), dtype=bool), 1)
        neg = -jnp.finfo(dots.dtype).max
        dots = jnp.where(causal, neg, dots)
        attn = jax.nn.softmax(dots, axis=-1)
        out = jnp.einsum('bhij,bhjd->bhid', attn, v)
        out = out.transpose(0, 2, 1, 3).reshape(b, n, INNER)
        out = jax.nn.relu(out @ W_o1) @ W_o2
        mean = jnp.mean(out, axis=-1, keepdims=True)
        var = jnp.var(out, axis=-1, keepdims=True)
        out = (out - mean) * jax.lax.rsqrt(var + 1e-05) * gamma
        return out

    def _L0_attn_b_ref(x, QK, VO):
        import jax, jax.numpy as jnp
        import numpy as np
        from math import sqrt
        D_MODEL = 128
        B, T = (4, 512)
        d_model = QK.shape[0]
        xQK = jnp.einsum('btd,de->bte', x, QK)
        scores = jnp.einsum('bte,bue->btu', xQK, x) / sqrt(d_model)
        attn = jax.nn.softmax(scores, axis=2)
        av = jnp.einsum('btu,bud->btd', attn, x)
        return jnp.einsum('btd,de->bte', av, VO)

    def _L0_ffn_ref(x, Wg, bg, W1, b1, W2, b2):
        import jax, jax.numpy as jnp
        import numpy as np
        B, S, D, H, E = (4, 256, 128, 512, 8)
        THRESHOLD = 0.5
        b, s, d = x.shape
        x_flat = x.reshape(-1, d)
        probs = jax.nn.sigmoid(x_flat @ Wg + bg)
        mask = (probs > THRESHOLD).astype(x_flat.dtype)
        weights = probs * mask
        h = jax.nn.relu(jnp.einsum('td,edh->eth', x_flat, W1) + b1[:, None, :])
        expert_out = jnp.einsum('eth,ehd->etd', h, W2) + b2[:, None, :]
        combined = jnp.einsum('te,etd->td', weights, expert_out)
        return combined.reshape(b, s, d)
    x = L0_attn_a_x
    x = x + _L0_attn_a_ref(_layernorm(x, axis=-1), L0_attn_a_W_qkv, L0_attn_a_W_o1, L0_attn_a_W_o2, L0_attn_a_gamma)
    x = x + _L0_ffn_ref(_layernorm(x, axis=-1), L0_ffn_Wg, L0_ffn_bg, L0_ffn_W1, L0_ffn_b1, L0_ffn_W2, L0_ffn_b2)
    x = x + _L0_attn_b_ref(_layernorm(x, axis=-1), L0_attn_b_QK, L0_attn_b_VO)
    x = x + _L0_ffn_ref(_layernorm(x, axis=-1), L0_ffn_Wg, L0_ffn_bg, L0_ffn_W1, L0_ffn_b1, L0_ffn_W2, L0_ffn_b2)
    return x

_drawn_inputs = setup_inputs


def setup_inputs(seed=0):
    import zlib

    import numpy as np

    out = dict(_drawn_inputs(seed))
    spreads = {'L0_attn_a_gamma': (1.0, 0.2)}
    factors = {}
    for name, (base, spread) in spreads.items():
        noise = np.random.default_rng([zlib.crc32(name.encode()), seed]).standard_normal(out[name].shape)
        drawn = base * np.exp(spread * noise) if base else spread * noise
        out[name] = jnp.asarray(drawn.astype(out[name].dtype))
    for name, factor in factors.items():
        out[name] = (out[name] * factor).astype(out[name].dtype)
    return out
```

```python
import numpy as np
import concourse.bass as bass
from concourse import mybir
from contextlib import ExitStack

F32 = mybir.dt.float32
F32R = mybir.dt.float32r
BF16 = mybir.dt.bfloat16
ALU = mybir.AluOpType
ACT = mybir.ActivationFunctionType
AX = mybir.AxisListType

P = 128
BANK = 512
BATCH, SEQ, DIM = 2, 1024, 128
TOKENS = BATCH * SEQ
TILES = TOKENS // P
SEQ_TILES = SEQ // P
CHUNKS = SEQ // BANK
ALL_CHUNKS = TOKENS // BANK
HEADS, HEAD_DIM = 16, 64
INNER = HEADS * HEAD_DIM
PAIRS = HEADS // 2
EXPERTS, HIDDEN = 8, 512
SLICES = HIDDEN // P
ALL_SLICES = EXPERTS * SLICES
EPS = 1e-5
MASKED = -1e30
THRESHOLD = 0.5


def counter(engine, sem):
    count = [0]

    def link(instruction):
        count[0] += 1
        instruction.then_inc(sem, 1)
        engine.wait_ge(sem, count[0])

    return link


class Memory:

    def __init__(self, nc, stack, prefix=""):
        self.nc, self.stack, self.prefix = nc, stack, prefix

    def sb(self, name, shape, dtype=F32):
        return self.stack.enter_context(self.nc.sbuf_tensor(self.prefix + name, shape, dtype))

    def ps(self, name, shape, dtype=F32):
        return self.stack.enter_context(self.nc.psum_tensor(self.prefix + name, shape, dtype))

    def sem(self, name):
        return self.stack.enter_context(self.nc.semaphore(self.prefix + name))


def row_statistics(nc, dve, link, source, stats, mean_var, count):
    for t in range(count):
        last = nc.vector.bn_stats(stats[:, t, :], source(t))
    link(last)
    for t in range(count):
        last = nc.vector.bn_aggr(mean_var[:, t, :], stats[:, t, :])
    link(last)


def reciprocal_deviation(nc, dve, link, mean_var, var_eps, var_ready, root, root_ready, rstd, scratch):
    nc.vector.tensor_scalar(var_eps[:], mean_var[:, :, 1], EPS, None, ALU.add).then_inc(var_ready, 1)
    dve.wait_ge(root_ready, 1)
    link(nc.vector.reciprocal(rstd[:], root[:]))
    link(nc.vector.tensor_tensor(scratch[:], rstd[:], rstd[:], ALU.mult))
    link(nc.vector.tensor_tensor(scratch[:], scratch[:], var_eps[:], ALU.mult))
    link(nc.vector.tensor_scalar(scratch[:], scratch[:], -0.5, 1.5, ALU.mult, ALU.add))
    link(nc.vector.tensor_tensor(rstd[:], rstd[:], scratch[:], ALU.mult))


def normalise_and_transpose(nc, x, xn, xT, xT_hi, xT_lo, ident, name, load=None):
    with ExitStack() as stack:
        m = Memory(nc, stack, name)
        stats = m.sb("stats", [P, TILES, 6])
        mean_var = m.sb("mean_var", [P, TILES, 2])
        var_eps = m.sb("var_eps", [P, TILES])
        root = m.sb("root", [P, TILES])
        rstd = m.sb("rstd", [P, TILES])
        scratch = m.sb("scratch", [P, TILES])
        turned = [m.ps(f"turned{i}", [P, BANK]) for i in range(ALL_CHUNKS)]
        loaded, chain, var_ready, root_ready, xn_ready, turned_ready, xT_ready, hi_ready = (
            m.sem(n) for n in ("loaded", "chain", "var_ready", "root_ready", "xn_ready", "turned_ready",
                               "xT_ready", "hi_ready"))
        block = stack.enter_context(nc.Block())
        need = [0]

        if load is not None:
            @block.sync
            def _(sync):
                need[0] = load(sync, loaded)

        @block.vector
        def _(dve):
            link = counter(dve, chain)
            if load is not None:
                dve.wait_ge(loaded, need[0])
            row_statistics(nc, dve, link, lambda t: x[:, t, :], stats, mean_var, TILES)
            reciprocal_deviation(nc, dve, link, mean_var, var_eps, var_ready, root, root_ready, rstd, scratch)
            for t in range(TILES):
                nc.vector.tensor_scalar(xn[:, t, :], x[:, t, :], mean_var[:, t, 0:1], rstd[:, t:t + 1],
                                        ALU.subtract, ALU.mult).then_inc(xn_ready, 1)
            for c in range(ALL_CHUNKS):
                part = slice(c * BANK, (c + 1) * BANK)
                dve.wait_ge(xT_ready, c + 1)
                nc.vector.tensor_copy(xT_hi[:, part], xT[:, part]).then_inc(hi_ready, 1)
                dve.wait_ge(hi_ready, c + 1)
                nc.vector.tensor_tensor(xT_lo[:, part], xT[:, part], xT_hi[:, part].bitcast(F32), ALU.subtract)

        @block.tensor
        def _(pe):
            for t in range(TILES):
                pe.wait_ge(xn_ready, t + 1)
                c, i = divmod(t, BANK // P)
                turn = nc.tensor.transpose(turned[c][:, i * P:(i + 1) * P], xn[:, t, :], ident[:])
                if i == BANK // P - 1:
                    turn.then_inc(turned_ready, 1)

        @block.scalar
        def _(act):
            act.wait_ge(var_ready, 1)
            nc.scalar.activation(root[:], var_eps[:], ACT.Sqrt).then_inc(root_ready, 1)
            for c in range(ALL_CHUNKS):
                act.wait_ge(turned_ready, c + 1)
                nc.scalar.activation(xT[:, c * BANK:(c + 1) * BANK], turned[c][:], ACT.Copy).then_inc(xT_ready, 1)


def causal_attention(nc, w_qkv, w_o1, cos_table, sin_table, xT_hi, xT_lo, ident, o1T):
    UNITS = BATCH * 2
    STEPS = UNITS * SEQ_TILES
    QUARTER = BANK // P
    fills_of = [i // QUARTER + 1 for i in range(SEQ_TILES)]
    FILLS = sum(fills_of)
    fill_at = [sum(fills_of[:i]) for i in range(SEQ_TILES)]
    PROJECTIONS = 10
    ROTATIONS = 4
    PROJECT_AT = {2: 0, 3: 1, 4: 2, 5: 3, 6: 4, 8: 5, 9: 6, 10: 7, 11: 8, 12: 9}
    OUT_LAST_AT, OUT_FIRST_AT = 7, 15
    BODY_UNITS = BATCH * (PROJECTIONS + CHUNKS)

    def uses(last):
        out = []
        for k in range(STEPS):
            b, at = divmod(k, 2 * SEQ_TILES)
            if at in PROJECT_AT and not (last and b == BATCH - 1):
                out.append((k, "project", PROJECT_AT[at], (b + 1) % BATCH))
            if at == OUT_LAST_AT and b > 0:
                out.append((k, "out", 1, b - 1))
            if at == OUT_FIRST_AT:
                out.append((k, "out", 0, b))
        out.append((STEPS, "out", 1, BATCH - 1))
        return out

    place = {(b, arg): n for n, (_, kind, arg, b) in enumerate(uses(False)) if kind == "project"}

    with ExitStack() as stack:
        m = Memory(nc, stack, "attn_")
        raw = m.sb("w_raw", [P, 5, P])
        w_hi = m.sb("w_hi", [P, 5, P], F32R)
        w_lo = m.sb("w_lo", [P, 5, P], F32R)
        wo1 = m.sb("wo1", [P, DIM])
        cos = m.sb("cos", [P, SEQ])
        sin = m.sb("sin", [P, SEQ])
        by_cos = [m.sb(f"by_cos{i}", [P, BANK]) for i in range(2)]
        by_sin = [m.sb(f"by_sin{i}", [P, BANK]) for i in range(2)]
        roped = [m.sb(f"roped{i}", [P, BANK]) for i in range(2)]
        roped_hi = [m.sb(f"roped_hi{i}", [P, BANK], F32R) for i in range(2)]
        roped_lo = [m.sb(f"roped_lo{i}", [P, BANK], F32R) for i in range(2)]
        q_stack = [[m.sb(f"q_stack{b}{h}", [P, SEQ], F32R) for h in range(2)] for b in range(BATCH)]
        k_hi = [[m.sb(f"k_hi{b}{h}", [P, SEQ], F32R) for h in range(2)] for b in range(BATCH)]
        k_lo = [[m.sb(f"k_lo{b}{h}", [P, SEQ], F32R) for h in range(2)] for b in range(BATCH)]
        values = [m.sb(f"values{b}", [P, SEQ_TILES, P]) for b in range(BATCH)]
        neg_max = m.sb("neg_max", [P, 4])
        sums = m.sb("sums", [P, 4])
        inverse = m.sb("inverse", [P, 4])
        probs = [m.sb(f"probs{i}", [P, SEQ]) for i in range(2)]
        probsT = [m.sb("probsT0", [P, QUARTER, BANK]), m.sb("probsT1", [P, 2 * QUARTER, BANK])]
        attended = [m.sb(f"attended{b}", [P, SEQ]) for b in range(BATCH)]
        ident16 = m.sb("ident16", [P, P], BF16)
        mask16 = m.sb("mask16", [P, P], BF16)
        scales = m.sb("scales", [P, 5, P])
        w_scaled = m.sb("w_scaled", [P, 5, P])

        scores = [m.ps(f"scores{i}", [P, SEQ]) for i in range(2)]
        turned = [m.ps(f"turned{i}", [P, QUARTER, P]) for i in range(2)]
        weighted = m.ps("weighted", [P, BANK])
        shared = m.ps("shared", [P, BANK])

        tables_in, w_in, wo1_in, masks, cleared = (m.sem(n) for n in ("tables_in", "w_in", "wo1_in", "masks", "cleared"))
        w_scaled_done, w_hi_done, w_lo_done = m.sem("w_scaled_done"), m.sem("w_hi_done"), m.sem("w_lo_done")
        shared_done, shared_free = m.sem("shared_done"), m.sem("shared_free")
        summed, hi_done, lo_done = (m.sem(n) for n in ("summed", "hi_done", "lo_done"))
        k_in, q_in = m.sem("k_in"), m.sem("q_in")
        scores_done, max_done, exp_done, inverse_done, normal_done = (
            m.sem(n) for n in ("scores_done", "max_done", "exp_done", "inverse_done", "normal_done"))
        fill_done, fill_copied, weighted_done, attended_done = (
            m.sem(n) for n in ("fill_done", "fill_copied", "weighted_done", "attended_done"))

        def loop(engine, body):
            with engine.Fori(0, PAIRS - 1) as pair:
                body(pair, False)
            body(PAIRS - 1, True)

        block = stack.enter_context(nc.Block())

        @block.sync
        def _(sync):
            def load_weights(pair):
                for j, part in enumerate((0, 1)):
                    src = w_qkv[:, bass.ds(pair * P + part * INNER, P)]
                    sync.dma_start(raw[:, j, :], src).then_inc(w_in, 16)
                    halves = src.rearrange("p (h s d) -> p h s d", h=2, s=2)
                    dst = raw[:, 2 + j, :].rearrange("p (h s d) -> p h s d", h=2, s=2)
                    for s in range(2):
                        sync.dma_start(dst[:, :, s, :], halves[:, :, 1 - s, :]).then_inc(w_in, 16)
                sync.dma_start(raw[:, 4, :], w_qkv[:, bass.ds(pair * P + 2 * INNER, P)]).then_inc(w_in, 16)

            def load_out_weights(pair):
                sync.dma_start(wo1[:], w_o1[bass.ds(pair * P, P), :]).then_inc(wo1_in, 16)

            def stack_phase(phase, b):
                for r in range(ROTATIONS):
                    c, is_q = divmod(r, 2)
                    sync.wait_ge(lo_done, phase * ROTATIONS + r + 1)
                    for h in range(2):
                        rows = slice(h * HEAD_DIM, (h + 1) * HEAD_DIM)
                        hi, lo = roped_hi[r % 2][rows, :].bitcast(F32), roped_lo[r % 2][rows, :].bitcast(F32)
                        cols = slice(c * BANK, (c + 1) * BANK)
                        for s in range(2):
                            half = slice(s * HEAD_DIM, (s + 1) * HEAD_DIM)
                            if is_q:
                                sync.dma_start(q_stack[b][h][half, cols].bitcast(F32), lo if s else hi).then_inc(q_in, 16)
                            else:
                                sync.dma_start(k_hi[b][h][half, cols].bitcast(F32), hi).then_inc(k_in, 16)
                                sync.dma_start(k_lo[b][h][half, cols].bitcast(F32), lo).then_inc(k_in, 16)

            load_weights(0)
            sync.dma_start(cos[:], cos_table).then_inc(tables_in, 16)
            sync.dma_start(sin[:], sin_table).then_inc(tables_in, 16)
            stack_phase(0, 0)

            def body(pair, is_last):
                sync.wait_ge(w_lo_done, pair + 1)
                if not is_last:
                    load_weights(pair + 1)
                sync.wait_ge(shared_done, PROJECTIONS + pair * BODY_UNITS)
                load_out_weights(pair)
                stack_phase(BATCH * pair + 1, 1)
                if not is_last:
                    sync.wait_ge(scores_done, pair * STEPS + 2 * SEQ_TILES)
                    stack_phase(BATCH * pair + 2, 0)

            loop(sync, body)

        @block.gpsimd
        def _(pool):
            nc.gpsimd.memset(ident16[:], 0.0).then_inc(cleared, 1)
            nc.gpsimd.memset(mask16[:], 0.0).then_inc(cleared, 1)
            nc.gpsimd.memset(o1T[:], 0.0).then_inc(cleared, 1)
            for j in range(5):
                nc.gpsimd.memset(scales[:, j, :], HEAD_DIM ** -0.5 if j in (0, 2) else 1.0).then_inc(cleared, 1)
            pool.wait_ge(cleared, 8)
            nc.gpsimd.affine_select(out=ident16[:], in_=ident16[:], compare_op=ALU.not_equal, fill=1.0, base=0,
                                    pattern=[[-1, P]], channel_multiplier=1).then_inc(masks, 1)
            nc.gpsimd.affine_select(out=mask16[:], in_=mask16[:], compare_op=ALU.is_ge, fill=MASKED, base=0,
                                    pattern=[[-1, P]], channel_multiplier=1).then_inc(masks, 1)

            def split_weights(pair):
                pool.wait_ge(w_in, (pair + 1) * 7 * 16)
                nc.gpsimd.tensor_tensor(w_hi[:], raw[:], scales[:], ALU.mult).then_inc(w_hi_done, 1)
                nc.gpsimd.tensor_tensor(w_scaled[:], raw[:], scales[:], ALU.mult).then_inc(w_scaled_done, 1)
                pool.wait_ge(w_hi_done, pair + 1)
                pool.wait_ge(w_scaled_done, pair + 1)
                nc.gpsimd.tensor_tensor(w_lo[:], w_scaled[:], w_hi[:].bitcast(F32), ALU.subtract).then_inc(w_lo_done, 1)

            def rope_phase(phase, used, at):
                for r in range(ROTATIONS):
                    n = phase * ROTATIONS + r
                    pool.wait_ge(shared_free, used + at[r] + 1)
                    nc.gpsimd.tensor_tensor(roped[r % 2][:], by_cos[r % 2][:], by_sin[r % 2][:],
                                            ALU.add).then_inc(summed, 1)
                    done = phase * 2 + r // 2
                    if r % 2:
                        pool.wait_ge(q_in, done * 4 * 16)
                    else:
                        pool.wait_ge(k_in, done * 8 * 16)
                    nc.gpsimd.tensor_tensor(roped_hi[r % 2][:], by_cos[r % 2][:], by_sin[r % 2][:],
                                            ALU.add).then_inc(hi_done, 1)
                    pool.wait_ge(summed, n + 1)
                    pool.wait_ge(hi_done, n + 1)
                    nc.gpsimd.tensor_tensor(roped_lo[r % 2][:], roped[r % 2][:], roped_hi[r % 2][:].bitcast(F32),
                                            ALU.subtract).then_inc(lo_done, 1)

            split_weights(0)
            rope_phase(0, 0, [2 * r + 1 for r in range(ROTATIONS)])

            def body(pair, is_last):
                used = PROJECTIONS + pair * BODY_UNITS
                rope_phase(BATCH * pair + 1, used, [place[1, 2 * r + 1] for r in range(ROTATIONS)])
                if not is_last:
                    pool.wait_ge(shared_done, PROJECTIONS + pair * BODY_UNITS + PROJECTIONS)
                    split_weights(pair + 1)
                    rope_phase(BATCH * pair + 2, used, [place[0, 2 * r + 1] for r in range(ROTATIONS)])

            loop(pool, body)

        @block.tensor
        def _(pe):
            def take_shared(n, first=False):
                if not first:
                    pe.wait_ge(shared_free, n)

            def project(j, b):
                if j < 8:
                    c, rest = divmod(j, 4)
                    is_q, is_rotated = divmod(rest, 2)
                    w = 2 * is_rotated + (0 if is_q else 1)
                    cols = slice(b * SEQ + c * BANK, b * SEQ + (c + 1) * BANK)
                    for n, (wt, xt) in enumerate(((w_hi, xT_hi), (w_hi, xT_lo), (w_lo, xT_hi))):
                        last = nc.tensor.matmul(shared[:], wt[:, w, :], xt[:, cols], start=n == 0, stop=n == 2)
                    last.then_inc(shared_done, 1)
                else:
                    for i in range(QUARTER):
                        t = (j - 8) * QUARTER + i
                        cols = slice(b * SEQ + t * P, b * SEQ + (t + 1) * P)
                        for n, (xt, wt) in enumerate(((xT_hi, w_hi), (xT_hi, w_lo), (xT_lo, w_hi))):
                            last = nc.tensor.matmul(shared[:, i * P:(i + 1) * P], xt[:, cols], wt[:, 4, :],
                                                    start=n == 0, stop=n == 2)
                    last.then_inc(shared_done, 1)

            def out_project(b, c):
                nc.tensor.matmul(shared[:], wo1[:], attended[b][:, c * BANK:(c + 1) * BANK],
                                 start=True, stop=True).then_inc(shared_done, 1)

            def score(k):
                unit, i = divmod(k, SEQ_TILES)
                b, h = divmod(unit, 2)
                cols = slice(i * P, (i + 1) * P)
                into = scores[k % 2]
                for c in range(i // QUARTER + 1):
                    keys = slice(c * BANK, min((c + 1) * BANK, (i + 1) * P))
                    diagonal = c == i // QUARTER
                    nc.tensor.matmul(into[:, keys], q_stack[b][h][:, cols], k_hi[b][h][:, keys], start=True, stop=False)
                    if diagonal:
                        nc.tensor.matmul(into[:, cols], ident16[:], mask16[:], start=False, stop=False)
                    last = nc.tensor.matmul(into[:, keys], q_stack[b][h][:, cols], k_lo[b][h][:, keys], start=False,
                                            stop=True)
                last.then_inc(scores_done, 1)

            def turn(pair, k):
                unit, i = divmod(k, SEQ_TILES)
                pe.wait_ge(normal_done, pair * STEPS + k + 1)
                for g in range(fills_of[i]):
                    fill = unit * FILLS + fill_at[i] + g
                    if fill >= 2:
                        pe.wait_ge(fill_copied, pair * UNITS * FILLS + fill - 1)
                    for kt in range(QUARTER * g, min(QUARTER * (g + 1), i + 1)):
                        last = nc.tensor.transpose(turned[fill % 2][:, kt - QUARTER * g, :],
                                                   probs[k % 2][:, kt * P:(kt + 1) * P], ident[:])
                    last.then_inc(fill_done, 1)

            def weigh(pair, unit, c, kts):
                b, h = divmod(unit, 2)
                top = QUARTER * (c + 1)
                if kts[0] == 0:
                    pe.wait_ge(fill_copied, pair * UNITS * FILLS + unit * FILLS + (FILLS if c else QUARTER))
                    copied = place[1, PROJECTIONS - 1] + 1 if b else 0
                    pe.wait_ge(shared_free, PROJECTIONS + pair * BODY_UNITS + copied)
                    if unit or c:
                        pe.wait_ge(attended_done, (pair * UNITS + unit) * CHUNKS + c)
                for kt in kts:
                    first = max(0, kt * P - c * BANK)
                    last = nc.tensor.matmul(weighted[:, first:], values[b][:, kt, :], probsT[c][:, kt, first:],
                                            start=kt == 0, stop=kt == top - 1)
                if kts[-1] == top - 1:
                    last.then_inc(weighted_done, 1)

            pe.wait_ge(w_lo_done, 1)
            for j in range(PROJECTIONS):
                take_shared(j, j == 0)
                project(j, 0)
            pe.wait_ge(masks, 2)
            pe.wait_ge(k_in, 2 * 8 * 16)
            pe.wait_ge(q_in, 2 * 4 * 16)
            score(0)

            def body(pair, is_last):
                step_uses = uses(is_last)
                used = [PROJECTIONS + pair * BODY_UNITS]

                def use_shared(k):
                    for at, kind, arg, b in step_uses:
                        if at != k:
                            continue
                        take_shared(used[0])
                        used[0] = used[0] + 1
                        if kind == "project":
                            if arg == 0 and b == 0:
                                pe.wait_ge(w_lo_done, pair + 2)
                            project(arg, b)
                        else:
                            pe.wait_ge(wo1_in, 16 * (pair + 1))
                            pe.wait_ge(attended_done, (pair * UNITS + 2 * b + 1) * CHUNKS + arg + 1)
                            out_project(b, arg)

                for k in range(STEPS):
                    unit, i = divmod(k, SEQ_TILES)
                    if k + 1 < STEPS or not is_last:
                        nxt = (k + 1) % STEPS
                        if nxt % (2 * SEQ_TILES) == 0:
                            phase = BATCH * pair + (k + 1) // (2 * SEQ_TILES)
                            pe.wait_ge(k_in, (phase + 1) * 2 * 8 * 16)
                            pe.wait_ge(q_in, (phase + 1) * 2 * 4 * 16)
                        if k > 0:
                            pe.wait_ge(exp_done, pair * STEPS + k)
                        score(nxt)
                    if k > 0:
                        turn(pair, k - 1)
                    if i in (5, 6):
                        weigh(pair, unit, 0, (0, 1) if i == 5 else (2, 3))
                    if unit > 0 and 1 <= i <= 4:
                        weigh(pair, unit - 1, 1, (2 * i - 2, 2 * i - 1))
                    use_shared(k)
                turn(pair, STEPS - 1)
                weigh(pair, UNITS - 1, 1, tuple(range(SEQ_TILES)))
                use_shared(STEPS)

            loop(pe, body)

        @block.vector
        def _(dve):
            def rotate(n, phase, j, b):
                r, is_sin = divmod(j, 2)
                c = r // 2
                dve.wait_ge(shared_done, n + 1)
                if not is_sin:
                    if phase is not None:
                        dve.wait_ge(hi_done, phase * ROTATIONS + r - 1)
                    elif r > 1:
                        dve.wait_ge(hi_done, r - 1)
                table, into = (sin, by_sin) if is_sin else (cos, by_cos)
                nc.vector.tensor_tensor(into[r % 2][:], shared[:], table[:, c * BANK:(c + 1) * BANK], ALU.mult)\
                  .then_inc(shared_free, 1)

            def maximum(k):
                n = (k % SEQ_TILES + 1) * P
                nc.vector.tensor_reduce(neg_max[:, k % 4:k % 4 + 1], scores[k % 2][:, 0:n], AX.X, ALU.max,
                                        negate=True).then_inc(max_done, 1)

            def accumulate(n, b, c):
                dve.wait_ge(shared_done, n + 1)
                part = slice(b * SEQ + c * BANK, b * SEQ + (c + 1) * BANK)
                nc.vector.tensor_tensor(o1T[:, part], o1T[:, part], shared[:], ALU.add).then_inc(shared_free, 1)

            dve.wait_ge(tables_in, 32)
            for j in range(8):
                rotate(j, None, j, 0)
            dve.wait_ge(cleared, 8)
            dve.wait_ge(scores_done, 1)
            maximum(0)

            def body(pair, is_last):
                step_uses = uses(is_last)
                used = [PROJECTIONS + pair * BODY_UNITS]
                for k in range(STEPS + 1):
                    if k < STEPS:
                        at = slice(k % 4, k % 4 + 1)
                        n = (k % SEQ_TILES + 1) * P
                        dve.wait_ge(exp_done, pair * STEPS + k + 1)
                        nc.vector.reciprocal(inverse[:, at], sums[:, at]).then_inc(inverse_done, 1)
                        if k + 1 < STEPS or not is_last:
                            dve.wait_ge(scores_done, pair * STEPS + k + 2)
                            maximum((k + 1) % STEPS)
                        dve.wait_ge(inverse_done, pair * STEPS + k + 1)
                        nc.vector.tensor_scalar(probs[k % 2][:, 0:n], probs[k % 2][:, 0:n], inverse[:, at], None,
                                                ALU.mult).then_inc(normal_done, 1)
                    for at_step, kind, arg, b in step_uses:
                        if at_step != k:
                            continue
                        if kind == "out":
                            accumulate(used[0], b, arg)
                        elif arg < 8:
                            rotate(used[0], BATCH * pair + (1 if b else 2), arg, b)
                        used[0] = used[0] + 1

            loop(dve, body)

        @block.scalar
        def _(act):
            def copy_values(n, j, b):
                act.wait_ge(shared_done, n + 1)
                into = values[b][:, (j - 8) * QUARTER:(j - 7) * QUARTER, :]
                nc.scalar.activation(into, shared[:].rearrange("p (t d) -> p t d", d=P), ACT.Copy)\
                  .then_inc(shared_free, 1)

            def exponentials(k, tile):
                act.wait_ge(max_done, tile + 1)
                n = (k % SEQ_TILES + 1) * P
                at = slice(k % 4, k % 4 + 1)
                nc.scalar.activation(probs[k % 2][:, 0:n], scores[k % 2][:, 0:n], ACT.Exp, bias=neg_max[:, at],
                                     accum_out=sums[:, at]).then_inc(exp_done, 1)

            def copy_turned(pair, k):
                unit, i = divmod(k, SEQ_TILES)
                c, t = divmod(i, QUARTER)
                if t == 0 and unit > 0:
                    act.wait_ge(weighted_done, (pair * UNITS + unit - 1) * CHUNKS + c + 1)
                for g in range(fills_of[i]):
                    fill = unit * FILLS + fill_at[i] + g
                    kts = min(QUARTER * (g + 1), i + 1) - QUARTER * g
                    act.wait_ge(fill_done, pair * UNITS * FILLS + fill + 1)
                    nc.scalar.activation(probsT[c][:, QUARTER * g:QUARTER * g + kts, t * P:(t + 1) * P],
                                         turned[fill % 2][:, 0:kts, :], ACT.Copy).then_inc(fill_copied, 1)

            def copy_weighted(pair, unit, c):
                b, h = divmod(unit, 2)
                rows = slice(h * HEAD_DIM, (h + 1) * HEAD_DIM)
                act.wait_ge(weighted_done, (pair * UNITS + unit) * CHUNKS + c + 1)
                nc.scalar.activation(attended[b][rows, c * BANK:(c + 1) * BANK], weighted[rows, :], ACT.Copy)\
                  .then_inc(attended_done, 1)

            for j in (8, 9):
                copy_values(j, j, 0)
            exponentials(0, 0)

            def body(pair, is_last):
                step_uses = uses(is_last)
                used = [PROJECTIONS + pair * BODY_UNITS]
                for k in range(STEPS):
                    unit, i = divmod(k, SEQ_TILES)
                    if k > 0:
                        copy_turned(pair, k - 1)
                    if k + 1 < STEPS or not is_last:
                        exponentials((k + 1) % STEPS, pair * STEPS + k + 1)
                    if i == 6:
                        copy_weighted(pair, unit, 0)
                    if i == 4 and unit > 0:
                        copy_weighted(pair, unit - 1, 1)
                    for at_step, kind, arg, b in step_uses:
                        if at_step == k:
                            if kind == "project" and arg >= 8:
                                copy_values(used[0], arg, b)
                            used[0] = used[0] + 1
                copy_turned(pair, STEPS - 1)
                copy_weighted(pair, UNITS - 1, 1)

            loop(act, body)


def project_out(nc, w_o2, gamma, o1T, x):
    with ExitStack() as stack:
        m = Memory(nc, stack, "out_")
        wo2 = m.sb("wo2", [P, DIM])
        gammas = m.sb("gammas", [P, DIM])
        stats = m.sb("stats", [P, TILES, 6])
        mean_var = m.sb("mean_var", [P, TILES, 2])
        var_eps = m.sb("var_eps", [P, TILES])
        root = m.sb("root", [P, TILES])
        rstd = m.sb("rstd", [P, TILES])
        scratch = m.sb("scratch", [P, TILES])
        y = m.sb("y", [P, TILES, DIM])
        product = [m.ps(f"product{c}", [P, BANK]) for c in range(ALL_CHUNKS)]
        loaded, chain, relu_done, product_done, var_ready, root_ready = (
            m.sem(n) for n in ("loaded", "chain", "relu_done", "product_done", "var_ready", "root_ready"))
        block = stack.enter_context(nc.Block())

        @block.sync
        def _(sync):
            sync.dma_start(wo2[:], w_o2).then_inc(loaded, 16)
            sync.dma_start(gammas[:], gamma.rearrange("(a n) -> a n", a=1).broadcast_to([P, DIM])).then_inc(loaded, 16)

        @block.tensor
        def _(pe):
            pe.wait_ge(loaded, 32)
            for t in range(TILES):
                c, i = divmod(t, BANK // P)
                pe.wait_ge(relu_done, c + 1)
                last = nc.tensor.matmul(product[c][:, i * P:(i + 1) * P], o1T[:, t * P:(t + 1) * P], wo2[:],
                                        start=True, stop=True)
                if i == BANK // P - 1:
                    last.then_inc(product_done, 1)

        @block.scalar
        def _(act):
            act.wait_ge(var_ready, 1)
            nc.scalar.activation(root[:], var_eps[:], ACT.Sqrt).then_inc(root_ready, 1)

        @block.vector
        def _(dve):
            link = counter(dve, chain)
            for c in range(ALL_CHUNKS):
                part = o1T[:, c * BANK:(c + 1) * BANK]
                nc.vector.tensor_scalar(part, part, 0.0, None, ALU.max).then_inc(relu_done, 1)

            def tile(t):
                c, i = divmod(t, BANK // P)
                return product[c][:, i * P:(i + 1) * P]

            dve.wait_ge(product_done, ALL_CHUNKS)
            row_statistics(nc, dve, link, tile, stats, mean_var, TILES)
            reciprocal_deviation(nc, dve, link, mean_var, var_eps, var_ready, root, root_ready, rstd, scratch)
            for t in range(TILES):
                last = nc.vector.tensor_scalar(y[:, t, :], tile(t), mean_var[:, t, 0:1], rstd[:, t:t + 1],
                                               ALU.subtract, ALU.mult)
            link(last)
            dve.wait_ge(loaded, 32)
            g = gammas[:].rearrange("p (a n) -> p a n", a=1).broadcast_to([P, TILES, DIM])
            link(nc.vector.tensor_tensor(y[:], y[:], g, ALU.mult))
            link(nc.vector.tensor_tensor(x[:], x[:], y[:], ALU.add))


def split_expert_weights(nc, w1, w2, w1_hi, w1_lo, w2_hi, w2_lo):
    PARTS = 4
    per = EXPERTS // PARTS
    with ExitStack() as stack:
        m = Memory(nc, stack, "split_")
        raw1 = m.sb("raw1", [P, EXPERTS, HIDDEN])
        raw2 = m.sb("raw2", [P, ALL_SLICES, DIM])
        in1 = [m.sem(f"in1_{i}") for i in range(PARTS)]
        in2 = [m.sem(f"in2_{i}") for i in range(PARTS)]
        hi_done = m.sem("hi_done")
        block = stack.enter_context(nc.Block())

        @block.sync
        def _(sync):
            for i in range(PARTS):
                e = slice(i * per, (i + 1) * per)
                sl = slice(i * per * SLICES, (i + 1) * per * SLICES)
                sync.dma_start(raw1[:, e, :], w1[e].rearrange("e d h -> d e h")).then_inc(in1[i], 16)
                sync.dma_start(raw2[:, sl, :], w2[e].rearrange("e (s h) d -> h (e s) d", h=P)).then_inc(in2[i], 16)

        @block.vector
        def _(dve):
            for i in range(PARTS):
                cols = slice(i * per * HIDDEN, (i + 1) * per * HIDDEN)
                for n, (raw, hi, lo, came) in enumerate(((raw1, w1_hi, w1_lo, in1), (raw2, w2_hi, w2_lo, in2))):
                    flat = raw[:].rearrange("p a b -> p (a b)")
                    dve.wait_ge(came[i], 16)
                    nc.vector.tensor_copy(hi[:, cols], flat[:, cols]).then_inc(hi_done, 1)
                    dve.wait_ge(hi_done, 2 * i + n + 1)
                    nc.vector.tensor_tensor(lo[:, cols], flat[:, cols], hi[:, cols].bitcast(F32), ALU.subtract)


def gate_experts(nc, wg, bg, b1, b2, xT, ident, gates_dram, b1T, sumT, name):
    with ExitStack() as stack:
        m = Memory(nc, stack, name)
        wg_sb = m.sb("wg", [P, EXPERTS])
        bg_sb = m.sb("bg", [P, EXPERTS])
        b1_rows = m.sb("b1_rows", [ALL_SLICES, P])
        b2_sb = m.sb("b2", [EXPERTS, DIM])
        logit = m.sb("logit", [P, TILES, EXPERTS])
        decay = m.sb("decay", [P, TILES, EXPERTS])
        prob = m.sb("prob", [P, TILES, EXPERTS])
        gate = m.sb("gate", [P, TILES, EXPERTS])
        gateT = m.sb("gateT", [EXPERTS, TOKENS])
        logit_ps = m.ps("logit_ps", [P, TILES, EXPERTS])
        b1_ps = m.ps("b1_ps", [P, ALL_SLICES])
        gate_ps = [m.ps(f"gate_ps{i}", [EXPERTS, BANK]) for i in range(ALL_CHUNKS)]
        bias_ps = [m.ps(f"bias_ps{i}", [P, BANK]) for i in range(2)]
        loaded, chain, logit_done, logit_read, decay_done, gate_done, turned, copied, biased, bias_copied, stored, b1_turned = (
            m.sem(n) for n in ("loaded", "chain", "logit_done", "logit_read", "decay_done", "gate_done", "turned",
                               "copied", "biased", "bias_copied", "stored", "b1_turned"))
        block = stack.enter_context(nc.Block())

        @block.sync
        def _(sync):
            sync.dma_start(wg_sb[:], wg).then_inc(loaded, 16)
            sync.dma_start(bg_sb[:], bg.rearrange("(a n) -> a n", a=1).broadcast_to([P, EXPERTS])).then_inc(loaded, 16)
            sync.dma_start(b1_rows[:], b1.rearrange("e (s h) -> (e s) h", h=P)).then_inc(loaded, 16)
            sync.dma_start(b2_sb[:], b2).then_inc(loaded, 16)
            sync.wait_ge(copied, ALL_CHUNKS)
            sync.dma_start(gates_dram, gateT[:]).then_inc(stored, 16)
            sync.wait_ge(stored, 16)

        @block.tensor
        def _(pe):
            pe.wait_ge(loaded, 64)
            for t in range(TILES):
                last = nc.tensor.matmul(logit_ps[:, t, :], xT[:, t * P:(t + 1) * P], wg_sb[:], start=True, stop=True)
            last.then_inc(logit_done, 1)
            nc.tensor.transpose(b1_ps[:], b1_rows[:], ident[0:ALL_SLICES, 0:ALL_SLICES]).then_inc(b1_turned, 1)
            pe.wait_ge(gate_done, 1)
            for t in range(TILES):
                c, i = divmod(t, BANK // P)
                last = nc.tensor.transpose(gate_ps[c][:, i * P:(i + 1) * P], gate[:, t, :], ident[:])
                if i == BANK // P - 1:
                    last.then_inc(turned, 1)
            for c in range(ALL_CHUNKS):
                pe.wait_ge(copied, c + 1)
                if c >= 2:
                    pe.wait_ge(bias_copied, c - 1)
                nc.tensor.matmul(bias_ps[c % 2][:], b2_sb[:], gateT[:, c * BANK:(c + 1) * BANK],
                                 start=True, stop=True).then_inc(biased, 1)

        @block.scalar
        def _(act):
            act.wait_ge(b1_turned, 1)
            nc.scalar.activation(b1T[:], b1_ps[:], ACT.Copy)
            act.wait_ge(logit_read, 1)
            nc.scalar.activation(decay[:], logit[:], ACT.Exp, scale=-1.0).then_inc(decay_done, 1)
            for c in range(ALL_CHUNKS):
                act.wait_ge(turned, c + 1)
                nc.scalar.activation(gateT[:, c * BANK:(c + 1) * BANK], gate_ps[c][:], ACT.Copy).then_inc(copied, 1)
            for c in range(ALL_CHUNKS):
                act.wait_ge(biased, c + 1)
                nc.scalar.activation(sumT[:, c * BANK:(c + 1) * BANK], bias_ps[c % 2][:], ACT.Copy).then_inc(bias_copied, 1)

        @block.vector
        def _(dve):
            link = counter(dve, chain)
            dve.wait_ge(logit_done, 1)
            bias = bg_sb[:].rearrange("p (a e) -> p a e", a=1).broadcast_to([P, TILES, EXPERTS])
            nc.vector.tensor_tensor(logit[:], logit_ps[:], bias, ALU.add).then_inc(logit_read, 1)
            dve.wait_ge(decay_done, 1)
            link(nc.vector.tensor_scalar(decay[:], decay[:], 1.0, None, ALU.add))
            link(nc.vector.reciprocal(prob[:], decay[:]))
            nc.vector.scalar_tensor_tensor(gate[:], logit[:], 0.0, prob[:], ALU.is_gt, ALU.mult).then_inc(gate_done, 1)


def feed_forward(nc, gates_dram, w1_hi, w1_lo, w2_hi, w2_lo, b1T, xT_hi, xT_lo, sumT, name):
    LAG, RING = 3, 4
    with ExitStack() as stack:
        m = Memory(nc, stack, name)
        gates = m.sb("gates", [P, EXPERTS, BANK])
        hidden = [m.sb(f"hidden{i}", [P, BANK]) for i in range(RING)]
        hidden_hi = [m.sb(f"hidden_hi{i}", [P, BANK], F32R) for i in range(RING)]
        hidden_lo = [m.sb(f"hidden_lo{i}", [P, BANK], F32R) for i in range(RING)]
        gated = [m.sb(f"gated{i}", [P, BANK]) for i in range(2)]
        up_ps = [m.ps(f"up{i}", [P, BANK]) for i in range(RING)]
        down_ps = [m.ps(f"down{i}", [P, BANK]) for i in range(2)]
        gates_in = [m.sem(f"gates_in{e}") for e in range(EXPERTS)]
        up_done, hi_done, relu_done, lo_done, down_done, gated_done, summed = (
            m.sem(n) for n in ("up_done", "hi_done", "relu_done", "lo_done", "down_done", "gated_done", "summed"))
        block = stack.enter_context(nc.Block())

        @block.sync
        def _(sync):
            def load_gates(chunk, e):
                rows = gates_dram[e:e + 1, bass.ds(chunk * BANK, BANK)].broadcast_to([P, BANK])
                sync.dma_start(gates[:, e, :], rows).then_inc(gates_in[e], 16)

            for e in range(EXPERTS):
                load_gates(0, e)
            with sync.Fori(0, ALL_CHUNKS - 1) as chunk:
                for e in range(EXPERTS):
                    sync.wait_ge(gated_done, chunk * EXPERTS + e + 1)
                    load_gates(chunk + 1, e)

        @block.tensor
        def _(pe):
            with pe.Fori(0, ALL_CHUNKS) as chunk:
                tokens = bass.ds(chunk * BANK, BANK)
                before = chunk * ALL_SLICES

                def up(n):
                    if n >= RING:
                        pe.wait_ge(relu_done, before + n - RING + 1)
                    w = slice(n * P, (n + 1) * P)
                    for i, (wt, xt) in enumerate(((w1_hi, xT_hi), (w1_hi, xT_lo), (w1_lo, xT_hi))):
                        last = nc.tensor.matmul(up_ps[n % RING][:], wt[:, w], xt[:, tokens], start=i == 0, stop=i == 2)
                    last.then_inc(up_done, 1)

                def down(n):
                    e, s = divmod(n, SLICES)
                    w = slice(n * P, (n + 1) * P)
                    pe.wait_ge(lo_done, before + n + 1)
                    if s == 0 and e >= 2:
                        pe.wait_ge(gated_done, chunk * EXPERTS + e - 1)
                    for i, (wt, ht) in enumerate(((w2_hi, hidden_hi), (w2_hi, hidden_lo), (w2_lo, hidden_hi))):
                        last = nc.tensor.matmul(down_ps[e % 2][:], wt[:, w], ht[n % RING][:],
                                                start=s == 0 and i == 0, stop=s == SLICES - 1 and i == 2)
                    last.then_inc(down_done, 1)

                for n in range(LAG):
                    up(n)
                for n in range(ALL_SLICES):
                    if n + LAG < ALL_SLICES:
                        up(n + LAG)
                    down(n)

        @block.scalar
        def _(act):
            with act.Fori(0, ALL_CHUNKS) as chunk:
                before = chunk * ALL_SLICES
                for n in range(ALL_SLICES):
                    act.wait_ge(up_done, before + n + 1)
                    if n >= RING:
                        act.wait_ge(down_done, before + n - RING + 1)
                    bias = b1T[:, n:n + 1]
                    nc.scalar.activation(hidden_hi[n % RING][:], up_ps[n % RING][:], ACT.Relu, bias=bias)\
                      .then_inc(hi_done, 1)
                    nc.scalar.activation(hidden[n % RING][:], up_ps[n % RING][:], ACT.Relu, bias=bias)\
                      .then_inc(relu_done, 1)

        @block.vector
        def _(dve):
            with dve.Fori(0, ALL_CHUNKS) as chunk:
                before = chunk * ALL_SLICES
                tokens = bass.ds(chunk * BANK, BANK)

                def combine(e):
                    dve.wait_ge(gates_in[e], (chunk + 1) * 16)
                    dve.wait_ge(down_done, before + (e + 1) * SLICES)
                    nc.vector.tensor_tensor(gated[e % 2][:], down_ps[e % 2][:], gates[:, e, :], ALU.mult)\
                      .then_inc(gated_done, 1)
                    dve.wait_ge(gated_done, chunk * EXPERTS + e + 1)
                    nc.vector.tensor_tensor(sumT[:, tokens], sumT[:, tokens], gated[e % 2][:], ALU.add)\
                      .then_inc(summed, 1)
                    dve.wait_ge(summed, chunk * EXPERTS + e + 1)

                for n in range(ALL_SLICES):
                    dve.wait_ge(hi_done, before + n + 1)
                    dve.wait_ge(relu_done, before + n + 1)
                    nc.vector.tensor_tensor(hidden_lo[n % RING][:], hidden[n % RING][:],
                                            hidden_hi[n % RING][:].bitcast(F32), ALU.subtract).then_inc(lo_done, 1)
                    if n >= 2 * SLICES - 1 and n % SLICES == SLICES - 1:
                        combine(n // SLICES - 1)
                combine(EXPERTS - 1)


def add_turned(nc, sumT, x, ident, name, out=None):
    with ExitStack() as stack:
        m = Memory(nc, stack, name)
        turned = [m.ps(f"turned{i}", [P, BANK]) for i in range(ALL_CHUNKS)]
        turn_done, added, stored = m.sem("turn_done"), m.sem("added"), m.sem("stored")
        block = stack.enter_context(nc.Block())
        per = BANK // P

        @block.tensor
        def _(pe):
            for t in range(TILES):
                c, i = divmod(t, per)
                last = nc.tensor.transpose(turned[c][:, i * P:(i + 1) * P], sumT[:, t * P:(t + 1) * P], ident[:])
                if i == per - 1:
                    last.then_inc(turn_done, 1)

        @block.vector
        def _(dve):
            for c in range(ALL_CHUNKS):
                dve.wait_ge(turn_done, c + 1)
                part = x[:, c * per:(c + 1) * per, :]
                nc.vector.tensor_tensor(part, part, turned[c][:].rearrange("p (t d) -> p t d", d=DIM), ALU.add)\
                  .then_inc(added, 1)

        if out is not None:
            @block.sync
            def _(sync):
                for c in range(ALL_CHUNKS):
                    sync.wait_ge(added, c + 1)
                    sync.dma_start(out[:, c * per:(c + 1) * per, :], x[:, c * per:(c + 1) * per, :]).then_inc(stored, 16)
                sync.wait_ge(stored, 16 * ALL_CHUNKS)


def full_attention(nc, qk, vo, xn, xT_hi, xT_lo, ident, x):
    QUARTER = BANK // P
    FILLS = SEQ_TILES // QUARTER
    PIECE = 2
    with ExitStack() as stack:
        m = Memory(nc, stack, "full_")
        qk_raw = m.sb("qk_raw", [P, DIM])
        qk_hi = m.sb("qk_hi", [P, DIM], F32R)
        qk_lo = m.sb("qk_lo", [P, DIM], F32R)
        vo_sb = m.sb("vo", [P, DIM])
        yT = m.sb("yT", [P, TOKENS])
        yT_hi = m.sb("yT_hi", [P, TOKENS], F32R)
        yT_lo = m.sb("yT_lo", [P, TOKENS], F32R)
        neg_max = m.sb("neg_max", [P, TILES])
        sums = m.sb("sums", [P, TILES])
        inverse = m.sb("inverse", [P, TILES])
        probs = [m.sb(f"probs{i}", [P, SEQ]) for i in range(2)]
        probsT = [m.sb(f"probsT{i}", [P, SEQ_TILES, BANK]) for i in range(2)]
        meanT = [m.sb(f"meanT{i}", [P, BANK]) for i in range(2)]
        scores = [m.ps(f"scores{i}", [P, SEQ]) for i in range(2)]
        turned = [m.ps(f"turned{i}", [P, QUARTER, P]) for i in range(2)]
        weighted = m.ps("weighted", [P, BANK])
        result = m.ps("result", [P, QUARTER, DIM])
        (loaded, qk_hi_done, qk_lo_done, y_done, y_copied, y_hi_done, y_lo_done, scores_done, max_done, exp_done,
         inverse_done, fill_done, fill_copied, weighted_done, mean_done, result_done, result_read) = (
            m.sem(n) for n in ("loaded", "qk_hi_done", "qk_lo_done", "y_done", "y_copied", "y_hi_done", "y_lo_done",
                               "scores_done", "max_done", "exp_done", "inverse_done", "fill_done", "fill_copied",
                               "weighted_done", "mean_done", "result_done", "result_read"))
        block = stack.enter_context(nc.Block())

        @block.sync
        def _(sync):
            sync.dma_start(qk_raw[:], qk).then_inc(loaded, 16)
            sync.dma_start(vo_sb[:], vo).then_inc(loaded, 16)

        @block.tensor
        def _(pe):
            pe.wait_ge(qk_lo_done, 1)
            for c in range(ALL_CHUNKS):
                part = slice(c * BANK, (c + 1) * BANK)
                into = scores[c // 2][:, (c % 2) * BANK:(c % 2 + 1) * BANK]
                for i, (wt, xt) in enumerate(((qk_hi, xT_hi), (qk_hi, xT_lo), (qk_lo, xT_hi))):
                    last = nc.tensor.matmul(into, wt[:], xt[:, part], start=i == 0, stop=i == 2)
                last.then_inc(y_done, 1)

            def score(k):
                b = k // SEQ_TILES
                cols = slice(k * P, (k + 1) * P)
                pe.wait_ge(y_lo_done, k // QUARTER + 1)
                pe.wait_ge(y_copied, 2 * (k % 2) + 2)
                if k >= 2:
                    pe.wait_ge(exp_done, k - 1)
                for c in range(CHUNKS):
                    keys = slice(b * SEQ + c * BANK, b * SEQ + (c + 1) * BANK)
                    for i, (yt, xt) in enumerate(((yT_hi, xT_hi), (yT_hi, xT_lo), (yT_lo, xT_hi))):
                        last = nc.tensor.matmul(scores[k % 2][:, c * BANK:(c + 1) * BANK], yt[:, cols], xt[:, keys],
                                                start=i == 0, stop=i == 2)
                last.then_inc(scores_done, 1)

            def turn(k):
                pe.wait_ge(exp_done, k + 1)
                for g in range(FILLS):
                    fill = k * FILLS + g
                    if fill >= 2:
                        pe.wait_ge(fill_copied, fill - 1)
                    for i in range(QUARTER):
                        kt = g * QUARTER + i
                        last = nc.tensor.transpose(turned[fill % 2][:, i, :], probs[k % 2][:, kt * P:(kt + 1) * P], ident[:])
                    last.then_inc(fill_done, 1)

            def weigh(j, piece):
                b = j // CHUNKS
                if piece == 0:
                    pe.wait_ge(fill_copied, (j + 1) * QUARTER * FILLS)
                    if j >= 1:
                        pe.wait_ge(mean_done, j)
                for kt in range(piece * PIECE, (piece + 1) * PIECE):
                    last = nc.tensor.matmul(weighted[:], xn[:, b * SEQ_TILES + kt, :], probsT[j % 2][:, kt, :],
                                            start=kt == 0, stop=kt == SEQ_TILES - 1)
                if piece == SEQ_TILES // PIECE - 1:
                    last.then_inc(weighted_done, 1)

            def multiply_out(j):
                pe.wait_ge(mean_done, j + 1)
                pe.wait_ge(loaded, 32)
                if j >= 1:
                    pe.wait_ge(result_read, j)
                for i in range(QUARTER):
                    last = nc.tensor.matmul(result[:, i, :], meanT[j % 2][:, i * P:(i + 1) * P], vo_sb[:],
                                            start=True, stop=True)
                last.then_inc(result_done, 1)

            score(0)
            for k in range(TILES + 2 * QUARTER):
                if k + 1 < TILES:
                    score(k + 1)
                if 1 <= k <= TILES:
                    turn(k - 1)
                j, piece = divmod(k - QUARTER - 1, QUARTER)
                if 0 <= j < ALL_CHUNKS:
                    weigh(j, piece)
                if piece == 1 and 0 <= j - 1 < ALL_CHUNKS:
                    multiply_out(j - 1)

        @block.vector
        def _(dve):
            dve.wait_ge(loaded, 32)
            nc.vector.tensor_copy(qk_hi[:], qk_raw[:]).then_inc(qk_hi_done, 1)
            dve.wait_ge(qk_hi_done, 1)
            nc.vector.tensor_tensor(qk_lo[:], qk_raw[:], qk_hi[:].bitcast(F32), ALU.subtract).then_inc(qk_lo_done, 1)
            for c in range(ALL_CHUNKS):
                part = slice(c * BANK, (c + 1) * BANK)
                dve.wait_ge(y_copied, c + 1)
                nc.vector.tensor_copy(yT_hi[:, part], yT[:, part]).then_inc(y_hi_done, 1)
                dve.wait_ge(y_hi_done, c + 1)
                nc.vector.tensor_tensor(yT_lo[:, part], yT[:, part], yT_hi[:, part].bitcast(F32),
                                        ALU.subtract).then_inc(y_lo_done, 1)

            def add_result(j):
                dve.wait_ge(result_done, j + 1)
                for i in range(QUARTER):
                    t = j * QUARTER + i
                    last = nc.vector.scalar_tensor_tensor(x[:, t, :], result[:, i, :], inverse[:, t:t + 1], x[:, t, :],
                                                          ALU.mult, ALU.add)
                last.then_inc(result_read, 1)

            for k in range(TILES + 2 * QUARTER):
                if k < TILES:
                    dve.wait_ge(scores_done, k + 1)
                    nc.vector.tensor_reduce(neg_max[:, k:k + 1], scores[k % 2][:], AX.X, ALU.max,
                                            negate=True).then_inc(max_done, 1)
                if 1 <= k <= TILES:
                    dve.wait_ge(exp_done, k)
                    nc.vector.reciprocal(inverse[:, k - 1:k], sums[:, k - 1:k]).then_inc(inverse_done, 1)
                j, piece = divmod(k - QUARTER - 1, QUARTER)
                if piece == 1 and 0 <= j - 1 < ALL_CHUNKS:
                    dve.wait_ge(inverse_done, j * QUARTER)
                    add_result(j - 1)

        @block.scalar
        def _(act):
            for c in range(ALL_CHUNKS):
                act.wait_ge(y_done, c + 1)
                nc.scalar.activation(yT[:, c * BANK:(c + 1) * BANK], scores[c // 2][:, (c % 2) * BANK:(c % 2 + 1) * BANK],
                                     ACT.Copy, scale=float(DIM) ** -0.5).then_inc(y_copied, 1)
            for k in range(TILES + 2 * QUARTER):
                if k < TILES:
                    act.wait_ge(max_done, k + 1)
                    nc.scalar.activation(probs[k % 2][:], scores[k % 2][:], ACT.Exp, bias=neg_max[:, k:k + 1],
                                         accum_out=sums[:, k:k + 1]).then_inc(exp_done, 1)
                if 1 <= k <= TILES:
                    j, t = divmod(k - 1, QUARTER)
                    if t == 0 and j >= 2:
                        act.wait_ge(weighted_done, j - 1)
                    for g in range(FILLS):
                        fill = (k - 1) * FILLS + g
                        act.wait_ge(fill_done, fill + 1)
                        nc.scalar.activation(probsT[j % 2][:, g * QUARTER:(g + 1) * QUARTER, t * P:(t + 1) * P],
                                             turned[fill % 2][:], ACT.Copy).then_inc(fill_copied, 1)
                j, piece = divmod(k - QUARTER - 1, QUARTER)
                if piece == QUARTER - 1 and 0 <= j < ALL_CHUNKS:
                    act.wait_ge(weighted_done, j + 1)
                    nc.scalar.activation(meanT[j % 2][:], weighted[:], ACT.Copy).then_inc(mean_done, 1)


def hybrid_layer(nc, x_dram, w_qkv, w_o1, w_o2, gamma, qk, vo, wg, bg, w1, b1, w2, b2, cos_table, sin_table, out, stop=9):
    x_rows = x_dram.rearrange("b (t p) d -> p (b t) d", p=P)
    out_rows = out.rearrange("b (t p) d -> p (b t) d", p=P)
    gates_dram = nc.dram_tensor("gates", (EXPERTS, TOKENS), F32, kind="Internal").ap()
    with ExitStack() as stack:
        m = Memory(nc, stack)
        ident = m.sb("ident", [P, P])
        x = m.sb("x", [P, TILES, DIM])
        xn = m.sb("xn", [P, TILES, DIM])
        xT = m.sb("xT", [P, TOKENS])
        xT_hi = m.sb("xT_hi", [P, TOKENS], F32R)
        xT_lo = m.sb("xT_lo", [P, TOKENS], F32R)
        sumT = m.sb("sumT", [P, TOKENS])
        ident_done, stored = m.sem("ident_done"), m.sem("stored")

        def normalise(name, load=None):
            normalise_and_transpose(nc, x, xn, xT, xT_hi, xT_lo, ident, name, load)

        def store():
            with nc.Block() as block:
                @block.sync
                def _(sync):
                    sync.dma_start(out_rows, x[:]).then_inc(stored, 16)
                    sync.wait_ge(stored, 16)

        def load_x(sync, loaded):
            sync.dma_start(x[:], x_rows).then_inc(loaded, 16)
            return 16

        with nc.Block() as block:
            @block.gpsimd
            def _(pool):
                nc.gpsimd.memset(ident[:], 0.0).then_inc(ident_done, 1)
                pool.wait_ge(ident_done, 1)
                nc.gpsimd.affine_select(out=ident[:], in_=ident[:], compare_op=ALU.not_equal, fill=1.0, base=0,
                                        pattern=[[-1, P]], channel_multiplier=1)

        normalise("ln1_", load_x)
        causal_attention(nc, w_qkv, w_o1, cos_table, sin_table, xT_hi, xT_lo, ident, sumT)
        project_out(nc, w_o2, gamma, sumT, x)
        if stop == 1:
            return store()
        w1_hi = m.sb("w1_hi", [P, EXPERTS * HIDDEN], F32R)
        w1_lo = m.sb("w1_lo", [P, EXPERTS * HIDDEN], F32R)
        w2_hi = m.sb("w2_hi", [P, ALL_SLICES * DIM], F32R)
        w2_lo = m.sb("w2_lo", [P, ALL_SLICES * DIM], F32R)
        b1T = m.sb("b1T", [P, ALL_SLICES])

        def feed(name, out=None):
            gate_experts(nc, wg, bg, b1, b2, xT, ident, gates_dram, b1T, sumT, name + "gate_")
            feed_forward(nc, gates_dram, w1_hi, w1_lo, w2_hi, w2_lo, b1T, xT_hi, xT_lo, sumT, name)
            add_turned(nc, sumT, x, ident, name + "add_", out)

        split_expert_weights(nc, w1, w2, w1_hi, w1_lo, w2_hi, w2_lo)
        normalise("ln2_")
        feed("ff1_")
        if stop == 2:
            return store()
        normalise("ln3_")
        full_attention(nc, qk, vo, xn, xT_hi, xT_lo, ident, x)
        if stop == 3:
            return store()
        normalise("ln4_")
        feed("ff2_", out_rows)


_INS = ['L0_attn_a_x', 'L0_attn_a_W_qkv', 'L0_attn_a_W_o1', 'L0_attn_a_W_o2', 'L0_attn_a_gamma', 'L0_attn_b_QK',
        'L0_attn_b_VO', 'L0_ffn_Wg', 'L0_ffn_bg', 'L0_ffn_W1', 'L0_ffn_b1', 'L0_ffn_W2', 'L0_ffn_b2']


def rotation_tables():
    inv_freq = (np.float32(1.0) / np.power(np.float32(10000.0),
                np.arange(0, HEAD_DIM, 2, dtype=np.float32) / np.float32(HEAD_DIM))).astype(np.float32)
    angle = inv_freq[:, None] * np.arange(SEQ, dtype=np.float32)[None, :]
    cos, sin = np.cos(angle), np.sin(angle)
    return np.concatenate([cos] * 4, 0), np.concatenate([-sin, sin] * 2, 0)


def kernel(**inputs):
    import concourse.bacc as bacc
    from concourse.bass_utils import run_bass_kernel_spmd

    nc = bacc.Bacc("TRN2", target_bir_lowering=False, num_devices=1)
    arrays, args = {}, []
    cos, sin = rotation_tables()
    for name, a in [(n, inputs[n]) for n in _INS] + [("cos_table", cos), ("sin_table", sin)]:
        a = np.ascontiguousarray(a)
        arrays[f"in_{name}"] = a
        args.append(nc.dram_tensor(f"in_{name}", a.shape, mybir.dt.from_np(a.dtype), kind="ExternalInput").ap())
    out = nc.dram_tensor("out_0", (BATCH, SEQ, DIM), F32, kind="ExternalOutput").ap()
    hybrid_layer(nc, *args, out)
    r = run_bass_kernel_spmd(nc, [arrays], core_ids=[0])
    return r.results[0]["out_0"]
```

```python
import numpy as np
import concourse.bass as bass
from concourse import mybir
from contextlib import ExitStack

F32 = mybir.dt.float32
F32R = mybir.dt.float32r
BF16 = mybir.dt.bfloat16
ALU = mybir.AluOpType
ACT = mybir.ActivationFunctionType
AX = mybir.AxisListType

P = 128
BANK = 512
BATCH, SEQ, DIM = 2, 1024, 128
TOKENS = BATCH * SEQ
TILES = TOKENS // P
SEQ_TILES = SEQ // P
CHUNKS = SEQ // BANK
ALL_CHUNKS = TOKENS // BANK
HEADS, HEAD_DIM = 16, 64
INNER = HEADS * HEAD_DIM
PAIRS = HEADS // 2
EXPERTS, HIDDEN = 8, 512
SLICES = HIDDEN // P
ALL_SLICES = EXPERTS * SLICES
EPS = 1e-5
MASKED = -1e30
THRESHOLD = 0.5


def counter(engine, sem):
    count = [0]

    def link(instruction):
        count[0] += 1
        instruction.then_inc(sem, 1)
        engine.wait_ge(sem, count[0])

    return link


def held(engine, value):
    return value if isinstance(value, int) else engine.snap(value)


def wait_count(engine, sem, count):
    if not isinstance(count, int) or count > 0:
        engine.wait_ge(sem, count)


class Memory:

    def __init__(self, nc, stack, prefix=""):
        self.nc, self.stack, self.prefix = nc, stack, prefix

    def sb(self, name, shape, dtype=F32):
        return self.stack.enter_context(self.nc.sbuf_tensor(self.prefix + name, shape, dtype))

    def ps(self, name, shape, dtype=F32):
        return self.stack.enter_context(self.nc.psum_tensor(self.prefix + name, shape, dtype))

    def sem(self, name):
        return self.stack.enter_context(self.nc.semaphore(self.prefix + name))


def row_statistics(nc, dve, link, source, stats, mean_var, count):
    for t in range(count):
        last = nc.vector.bn_stats(stats[:, t, :], source(t))
    link(last)
    for t in range(count):
        last = nc.vector.bn_aggr(mean_var[:, t, :], stats[:, t, :])
    link(last)


def reciprocal_deviation(nc, dve, link, mean_var, var_eps, var_ready, root, root_ready, rstd, scratch):
    nc.vector.tensor_scalar(var_eps[:], mean_var[:, :, 1], EPS, None, ALU.add).then_inc(var_ready, 1)
    dve.wait_ge(root_ready, 1)
    link(nc.vector.reciprocal(rstd[:], root[:]))
    link(nc.vector.tensor_tensor(scratch[:], rstd[:], rstd[:], ALU.mult))
    link(nc.vector.tensor_tensor(scratch[:], scratch[:], var_eps[:], ALU.mult))
    link(nc.vector.tensor_scalar(scratch[:], scratch[:], -0.5, 1.5, ALU.mult, ALU.add))
    link(nc.vector.tensor_tensor(rstd[:], rstd[:], scratch[:], ALU.mult))


def normalise_and_transpose(nc, x, xn, xT, xT_hi, xT_lo, ident, name, load=None):
    with ExitStack() as stack:
        m = Memory(nc, stack, name)
        stats = m.sb("stats", [P, TILES, 6])
        mean_var = m.sb("mean_var", [P, TILES, 2])
        var_eps = m.sb("var_eps", [P, TILES])
        root = m.sb("root", [P, TILES])
        rstd = m.sb("rstd", [P, TILES])
        scratch = m.sb("scratch", [P, TILES])
        turned = [m.ps(f"turned{i}", [P, BANK]) for i in range(ALL_CHUNKS)]
        loaded, chain, var_ready, root_ready, xn_ready, turned_ready, xT_ready, hi_ready = (
            m.sem(n) for n in ("loaded", "chain", "var_ready", "root_ready", "xn_ready", "turned_ready",
                               "xT_ready", "hi_ready"))
        block = stack.enter_context(nc.Block())
        need = [0]

        if load is not None:
            @block.sync
            def _(sync):
                need[0] = load(sync, loaded)

        @block.vector
        def _(dve):
            link = counter(dve, chain)
            if load is not None:
                dve.wait_ge(loaded, need[0])
            row_statistics(nc, dve, link, lambda t: x[:, t, :], stats, mean_var, TILES)
            reciprocal_deviation(nc, dve, link, mean_var, var_eps, var_ready, root, root_ready, rstd, scratch)
            for t in range(TILES):
                nc.vector.tensor_scalar(xn[:, t, :], x[:, t, :], mean_var[:, t, 0:1], rstd[:, t:t + 1],
                                        ALU.subtract, ALU.mult).then_inc(xn_ready, 1)
            for c in range(ALL_CHUNKS):
                part = slice(c * BANK, (c + 1) * BANK)
                dve.wait_ge(xT_ready, c + 1)
                nc.vector.tensor_copy(xT_hi[:, part], xT[:, part]).then_inc(hi_ready, 1)
                dve.wait_ge(hi_ready, c + 1)
                nc.vector.tensor_tensor(xT_lo[:, part], xT[:, part], xT_hi[:, part].bitcast(F32), ALU.subtract)

        @block.tensor
        def _(pe):
            for t in range(TILES):
                pe.wait_ge(xn_ready, t + 1)
                c, i = divmod(t, BANK // P)
                turn = nc.tensor.transpose(turned[c][:, i * P:(i + 1) * P], xn[:, t, :], ident[:])
                if i == BANK // P - 1:
                    turn.then_inc(turned_ready, 1)

        @block.scalar
        def _(act):
            act.wait_ge(var_ready, 1)
            nc.scalar.activation(root[:], var_eps[:], ACT.Sqrt).then_inc(root_ready, 1)
            for c in range(ALL_CHUNKS):
                act.wait_ge(turned_ready, c + 1)
                nc.scalar.activation(xT[:, c * BANK:(c + 1) * BANK], turned[c][:], ACT.Copy).then_inc(xT_ready, 1)


def causal_attention(nc, w_qkv, w_o1, cos_table, sin_table, xT_hi, xT_lo, ident, o1T):
    UNITS = BATCH * 2
    PHASE = 2 * SEQ_TILES
    STEPS = BATCH * PHASE
    QUARTER = BANK // P
    RING = 4
    ORDER = (0, 1, 4, 2, 5, 3, 6, 7)
    CHUNK_AT = (ORDER.index(QUARTER - 1) + 1, SEQ_TILES)
    fills_of = [i // QUARTER + 1 for i in ORDER]
    fills = [(at, g) for at in range(SEQ_TILES) for g in range(fills_of[at])]
    FILLS = len(fills)
    LONG = FILLS - SEQ_TILES
    fill_at = [sum(fills_of[:i]) for i in range(SEQ_TILES + 1)]
    long_at = [fill_at[i] - i for i in range(SEQ_TILES + 1)]
    ROTATIONS = 4
    PROJECTIONS = ROTATIONS + 2
    SHARED_AT = {0: ("project", 0), 1: ("turn", 0), 2: ("project", 1), 3: ("out", 0), 4: ("turn", 1),
                 5: ("project", 2), 6: ("out", 1), 7: ("project", 3), 9: ("project", 4), 11: ("project", 5)}
    ROTATED_AT = {4: 0, 7: 1, 10: 2, 12: 3}
    SPLIT_AT = 12
    HALF = HEAD_DIM // 2

    def uses(first, last):
        out = []
        for k in range(STEPS):
            b, at = divmod(k, PHASE)
            if at in SHARED_AT:
                kind, arg = SHARED_AT[at]
                if kind == "project" and not (last and b == BATCH - 1):
                    out.append((k, kind, arg, (b + 1) % BATCH))
                if kind != "project" and not (first and b == 0):
                    out.append((k, kind, arg, (b - 1) % BATCH))
        return out

    BODY_USES = len(uses(False, False))

    def used_before(pair, first=False):
        return PROJECTIONS if first else PROJECTIONS + len(uses(True, False)) + (pair - 1) * BODY_USES

    def places(first, last):
        return {use[1:]: n for n, use in enumerate(uses(first, last))}

    with ExitStack() as stack:
        m = Memory(nc, stack, "attn_")
        raw = m.sb("w_raw", [P, 3, P])
        w_hi = m.sb("w_hi", [P, 3, P], F32R)
        w_lo = m.sb("w_lo", [P, 3, P], F32R)
        wo1 = m.sb("wo1", [P, DIM])
        cos = m.sb("cos", [P, SEQ])
        sin = m.sb("sin", [P, SEQ])
        plain = [m.sb(f"plain{i}", [P, BANK]) for i in range(2)]
        swapped = [m.sb(f"swapped{i}", [P, BANK]) for i in range(2)]
        by_cos = [m.sb(f"by_cos{i}", [P, BANK]) for i in range(2)]
        by_sin = m.sb("by_sin", [P, BANK])
        roped = [m.sb(f"roped{i}", [P, BANK]) for i in range(2)]
        halves = [m.sb(f"halves{i}", [P, 2, BANK], F32R) for i in range(2)]
        q_stack = [[m.sb(f"q_stack{b}{h}", [P, SEQ], F32R) for h in range(2)] for b in range(BATCH)]
        k_stack = [[m.sb(f"k_stack{b}{h}", [P, 2, SEQ], F32R) for h in range(2)] for b in range(BATCH)]
        values = [m.sb(f"values{b}", [P, SEQ_TILES, P]) for b in range(BATCH)]
        neg_max = m.sb("neg_max", [P, RING])
        sums = m.sb("sums", [P, RING])
        inverse = m.sb("inverse", [P, RING])
        probs = [m.sb(f"probs{i}", [P, SEQ]) for i in range(RING)]
        probsT = [m.sb(f"probsT{i}", [P, SEQ_TILES, P]) for i in range(2)]
        attended = [m.sb(f"attended{b}", [P, SEQ_TILES, P]) for b in range(BATCH)]
        attendedT = [m.sb(f"attendedT{c}", [P, BANK]) for c in range(CHUNKS)]
        ident16 = m.sb("ident16", [P, P], BF16)
        mask16 = m.sb("mask16", [P, P], BF16)

        scores = [m.ps(f"scores{i}", [P, SEQ]) for i in range(2)]
        turned = [m.ps(f"turned{i}", [P, QUARTER, P]) for i in range(2)]
        weighted = m.ps("weighted", [P, HEAD_DIM])
        shared = m.ps("shared", [P, BANK])

        tables_in, w_in, wo1_in, masks, cleared = (m.sem(n) for n in ("tables_in", "w_in", "wo1_in", "masks", "cleared"))
        w_hi_done, w_lo_done = m.sem("w_hi_done"), m.sem("w_lo_done")
        shared_done, shared_free = m.sem("shared_done"), m.sem("shared_free")
        swapped_in = [m.sem(f"swapped_in{i}") for i in range(2)]
        cos_done, sin_done, summed, hi_done, lo_done = (
            m.sem(n) for n in ("cos_done", "sin_done", "summed", "hi_done", "lo_done"))
        k_in, q_in = m.sem("k_in"), m.sem("q_in")
        scores_done, max_done, exp_done, inverse_done = (
            m.sem(n) for n in ("scores_done", "max_done", "exp_done", "inverse_done"))
        fill_done, low_copied, high_copied, weighted_done, attended_done = (
            m.sem(n) for n in ("fill_done", "low_copied", "high_copied", "weighted_done", "attended_done"))

        def loop(engine, body):
            body(0, True, False)
            with engine.Fori(1, PAIRS - 1) as pair:
                body(pair, False, False)
            body(PAIRS - 1, False, True)

        def low_copies(pair, k):
            return pair * STEPS + k + 1

        def high_copies(pair, k):
            unit, at = divmod(k, SEQ_TILES)
            return pair * UNITS * LONG + unit * LONG + long_at[at + 1]

        def fills_before(pair, k):
            unit, at = divmod(k, SEQ_TILES)
            return pair * UNITS * FILLS + unit * FILLS + fill_at[at]

        block = stack.enter_context(nc.Block())

        @block.sync
        def _(sync):
            def load_weights(pair):
                for j in range(3):
                    sync.dma_start(raw[:, j, :], w_qkv[:, bass.ds(pair * P + j * INNER, P)]).then_inc(w_in, 16)

            def swap(phase, r, used):
                copied = held(sync, used + 1)
                again = r > 1 or phase is not None
                multiplied = held(sync, (0 if phase is None else phase * ROTATIONS) + r - 1) if again else None
                sync.wait_ge(shared_free, copied)
                if again:
                    sync.wait_ge(sin_done, multiplied)
                for j in range(P // HALF):
                    sync.dma_start(swapped[r % 2][j * HALF:(j + 1) * HALF, :],
                                   plain[r % 2][(j ^ 1) * HALF:((j ^ 1) + 1) * HALF, :]).then_inc(swapped_in[r % 2], 16)

            def stack_rotation(phase, r, b):
                c, is_q = divmod(r, 2)
                sync.wait_ge(lo_done, phase * ROTATIONS + r + 1)
                cols = slice(c * BANK, (c + 1) * BANK)
                for h in range(2):
                    rows = slice(h * HEAD_DIM, (h + 1) * HEAD_DIM)
                    for s in range(2):
                        half = slice(s * HEAD_DIM, (s + 1) * HEAD_DIM)
                        if is_q:
                            sync.dma_start(q_stack[b][h][half, cols].bitcast(F32),
                                           halves[r % 2][rows, s, :].bitcast(F32)).then_inc(q_in, 16)
                        else:
                            sync.dma_start(k_stack[b][h][half, :, cols].bitcast(F32),
                                           halves[r % 2][rows, :, :].bitcast(F32)).then_inc(k_in, 16)

            def move_phase(phase, b, used):
                started = None if isinstance(phase, int) and phase == 0 else phase
                swap(started, 0, used[0])
                for r in range(ROTATIONS):
                    if r + 1 < ROTATIONS:
                        swap(started, r + 1, used[r + 1])
                    stack_rotation(phase, r, b)

            load_weights(0)
            sync.dma_start(cos[:], cos_table).then_inc(tables_in, 16)
            sync.dma_start(sin[:], sin_table).then_inc(tables_in, 16)
            move_phase(0, 0, list(range(ROTATIONS)))

            def body(pair, first, last):
                place, used = places(first, last), used_before(pair, first)
                sync.wait_ge(w_lo_done, pair + 1)
                if not last:
                    load_weights(pair + 1)
                move_phase(BATCH * pair + 1, 1, [used + place["project", r, 1] for r in range(ROTATIONS)])
                if not first:
                    sync.wait_ge(shared_done, used + place["out", 1, 1] + 1)
                sync.dma_start(wo1[:], w_o1[bass.ds(pair * P, P), :]).then_inc(wo1_in, 16)
                if not last:
                    move_phase(BATCH * pair + 2, 0, [used + place["project", r, 0] for r in range(ROTATIONS)])

            loop(sync, body)

        @block.gpsimd
        def _(pool):
            nc.gpsimd.memset(ident16[:], 0.0).then_inc(cleared, 1)
            nc.gpsimd.memset(mask16[:], 0.0).then_inc(cleared, 1)
            nc.gpsimd.memset(o1T[:], 0.0).then_inc(cleared, 1)
            pool.wait_ge(cleared, 3)
            nc.gpsimd.affine_select(out=ident16[:], in_=ident16[:], compare_op=ALU.not_equal, fill=1.0, base=0,
                                    pattern=[[-1, P]], channel_multiplier=1).then_inc(masks, 1)
            nc.gpsimd.affine_select(out=mask16[:], in_=mask16[:], compare_op=ALU.is_ge, fill=MASKED, base=0,
                                    pattern=[[-1, P]], channel_multiplier=1).then_inc(masks, 1)

            def rope_phase(phase, used):
                for r in range(ROTATIONS):
                    n = phase * ROTATIONS + r
                    part = slice(r // 2 * BANK, (r // 2 + 1) * BANK)
                    pool.wait_ge(shared_free, used[r] + 1)
                    if isinstance(phase, int) and phase == 0 and r > 1:
                        pool.wait_ge(summed, r - 1)
                    nc.gpsimd.tensor_tensor(by_cos[r % 2][:], plain[r % 2][:], cos[:, part], ALU.mult)\
                      .then_inc(cos_done, 1)
                    if isinstance(phase, int) and phase == 0:
                        continue
                    pool.wait_ge(swapped_in[r % 2], (phase * 2 + r // 2 + 1) * (P // HALF) * 16)
                    pool.wait_ge(summed, n)
                    nc.gpsimd.tensor_tensor(by_sin[:], swapped[r % 2][:], sin[:, part], ALU.mult).then_inc(sin_done, 1)
                    pool.wait_ge(lo_done, n - 1)
                    pool.wait_ge(cos_done, n + 1)
                    pool.wait_ge(sin_done, n + 1)
                    nc.gpsimd.tensor_tensor(roped[r % 2][:], by_cos[r % 2][:], by_sin[:], ALU.add).then_inc(summed, 1)

            pool.wait_ge(tables_in, 32)
            rope_phase(0, list(range(ROTATIONS)))
            pool.wait_ge(summed, ROTATIONS)

            def body(pair, first, last):
                place, used = places(first, last), used_before(pair, first)
                rope_phase(BATCH * pair + 1, [used + place["project", r, 1] for r in range(ROTATIONS)])
                if not last:
                    rope_phase(BATCH * pair + 2, [used + place["project", r, 0] for r in range(ROTATIONS)])

            loop(pool, body)

        @block.tensor
        def _(pe):
            def take_shared(n, first=False):
                if not first:
                    pe.wait_ge(shared_free, n)

            def project(j, b):
                if j < ROTATIONS:
                    c, is_q = divmod(j, 2)
                    w = 0 if is_q else 1
                    cols = slice(b * SEQ + c * BANK, b * SEQ + (c + 1) * BANK)
                    for n, (wt, xt) in enumerate(((w_hi, xT_hi), (w_hi, xT_lo), (w_lo, xT_hi))):
                        last = nc.tensor.matmul(shared[:], wt[:, w, :], xt[:, cols], start=n == 0, stop=n == 2)
                    last.then_inc(shared_done, 1)
                else:
                    for i in range(QUARTER):
                        t = (j - ROTATIONS) * QUARTER + i
                        cols = slice(b * SEQ + t * P, b * SEQ + (t + 1) * P)
                        for n, (xt, wt) in enumerate(((xT_hi, w_hi), (xT_hi, w_lo), (xT_lo, w_hi))):
                            last = nc.tensor.matmul(shared[:, i * P:(i + 1) * P], xt[:, cols], wt[:, 2, :],
                                                    start=n == 0, stop=n == 2)
                    last.then_inc(shared_done, 1)

            def turn_attended(pair, n, b, c):
                take_shared(n)
                pe.wait_ge(attended_done, pair * STEPS + b * PHASE + SEQ_TILES + CHUNK_AT[c])
                for i in range(QUARTER):
                    last = nc.tensor.transpose(shared[:, i * P:(i + 1) * P], attended[b][:, c * QUARTER + i, :], ident[:])
                last.then_inc(shared_done, 1)

            def multiply_out(pair, n, c):
                take_shared(n)
                pe.wait_ge(wo1_in, 16 * (pair + 1))
                nc.tensor.matmul(shared[:], wo1[:], attendedT[c][:], start=True, stop=True).then_inc(shared_done, 1)

            def score(k):
                unit, at = divmod(k, SEQ_TILES)
                i = ORDER[at]
                b, h = divmod(unit, 2)
                cols = slice(i * P, (i + 1) * P)
                into = scores[k % 2]
                for c in range(i // QUARTER + 1):
                    keys = slice(c * BANK, min((c + 1) * BANK, (i + 1) * P))
                    diagonal = c == i // QUARTER
                    nc.tensor.matmul(into[:, keys], q_stack[b][h][:, cols], k_stack[b][h][:, 0, keys], start=True, stop=False)
                    if diagonal:
                        nc.tensor.matmul(into[:, cols], ident16[:], mask16[:], start=False, stop=False)
                    last = nc.tensor.matmul(into[:, keys], q_stack[b][h][:, cols], k_stack[b][h][:, 1, keys], start=False,
                                            stop=True)
                last.then_inc(scores_done, 1)

            def turn(pair, k):
                unit, at = divmod(k, SEQ_TILES)
                for g in range(fills_of[at]):
                    back, place = divmod(fill_at[at] + g - 2, FILLS)
                    old_at, old_g = fills[place]
                    old = (unit + back) * SEQ_TILES + old_at
                    if old_g:
                        wait_count(pe, high_copied, high_copies(pair, old))
                    else:
                        wait_count(pe, low_copied, low_copies(pair, old))
                    for kt in range(QUARTER * g, min(QUARTER * (g + 1), ORDER[at] + 1)):
                        last = nc.tensor.transpose(turned[(fill_at[at] + g) % 2][:, kt - QUARTER * g, :],
                                                   probs[k % RING][:, kt * P:(kt + 1) * P], ident[:])
                    last.then_inc(fill_done, 1)

            def weigh(pair, k, values_copied=None):
                unit, at = divmod(k, SEQ_TILES)
                b, h = divmod(unit % UNITS, 2)
                if values_copied is not None:
                    pe.wait_ge(shared_free, values_copied)
                wait_count(pe, attended_done, pair * STEPS + k)
                pe.wait_ge(low_copied, low_copies(pair, k))
                for kt in range(ORDER[at] + 1):
                    if kt == QUARTER:
                        pe.wait_ge(high_copied, high_copies(pair, k))
                    last = nc.tensor.matmul(weighted[:], probsT[k % 2][:, kt, :],
                                            values[b][:, kt, h * HEAD_DIM:(h + 1) * HEAD_DIM],
                                            start=kt == 0, stop=kt == ORDER[at])
                last.then_inc(weighted_done, 1)

            pe.wait_ge(w_lo_done, 1)
            for j in range(PROJECTIONS):
                take_shared(j, j == 0)
                project(j, 0)
            pe.wait_ge(masks, 2)
            pe.wait_ge(k_in, 2 * 4 * 16)
            pe.wait_ge(q_in, 2 * 4 * 16)
            score(0)

            def body(pair, first, last):
                step_uses, place, used = uses(first, last), places(first, last), used_before(pair, first)
                for k in range(STEPS):
                    if k > 0 or not first:
                        pe.wait_ge(exp_done, pair * STEPS + k)
                    if k + 1 < STEPS or not last:
                        if (k + 1) % PHASE == 0:
                            phase = BATCH * pair + (k + 1) // PHASE
                            pe.wait_ge(k_in, (phase + 1) * 2 * 4 * 16)
                            pe.wait_ge(q_in, (phase + 1) * 2 * 4 * 16)
                        score((k + 1) % STEPS)
                    if k > 0 or not first:
                        turn(pair, k - 1)
                    if k > 1 or not first:
                        if k - 2 == 0 and first:
                            copied = PROJECTIONS
                        elif k - 2 == 0:
                            copied = used - BODY_USES + places(False, False)["project", PROJECTIONS - 1, 0] + 1
                        elif k - 2 == PHASE:
                            copied = used + place["project", PROJECTIONS - 1, 1] + 1
                        else:
                            copied = None
                        weigh(pair, k - 2, copied)
                    for n, (at_step, kind, arg, b) in enumerate(step_uses):
                        if at_step != k:
                            continue
                        owner = pair if k >= PHASE else pair - 1
                        if kind == "turn":
                            turn_attended(owner, used + n, b, arg)
                        elif kind == "out":
                            multiply_out(owner, used + n, arg)
                        else:
                            take_shared(used + n)
                            if arg == 0 and b == 0:
                                pe.wait_ge(w_lo_done, pair + 2)
                            project(arg, b)

            def finish():
                used = used_before(PAIRS - 1) + len(uses(False, True))
                pe.wait_ge(exp_done, PAIRS * STEPS)
                turn(PAIRS, -1)
                weigh(PAIRS, -2)
                weigh(PAIRS, -1)
                for c in range(CHUNKS):
                    turn_attended(PAIRS - 1, used + 2 * c, BATCH - 1, c)
                    multiply_out(PAIRS - 1, used + 2 * c + 1, c)

            loop(pe, body)
            finish()

        @block.vector
        def _(dve):
            def split_weights(pair):
                dve.wait_ge(w_in, (pair + 1) * 3 * 16)
                nc.vector.tensor_copy(w_hi[:], raw[:]).then_inc(w_hi_done, 1)
                dve.wait_ge(w_hi_done, pair + 1)
                nc.vector.tensor_tensor(w_lo[:], raw[:], w_hi[:].bitcast(F32), ALU.subtract).then_inc(w_lo_done, 1)

            def split_rotation(phase, r):
                n = phase * ROTATIONS + r
                dve.wait_ge(summed, n + 1)
                if not (isinstance(phase, int) and phase == 0 and r < 2):
                    dve.wait_ge(q_in if r % 2 else k_in, (phase * 2 + r // 2) * 4 * 16)
                nc.vector.tensor_copy(halves[r % 2][:, 0, :], roped[r % 2][:]).then_inc(hi_done, 1)
                dve.wait_ge(hi_done, n + 1)
                nc.vector.tensor_tensor(halves[r % 2][:, 1, :], roped[r % 2][:], halves[r % 2][:, 0, :].bitcast(F32),
                                        ALU.subtract).then_inc(lo_done, 1)

            def copy_turned(pair, k):
                at = k % SEQ_TILES
                kts = min(QUARTER, ORDER[at] + 1)
                dve.wait_ge(fill_done, fills_before(pair, k) + 1)
                nc.vector.tensor_copy(probsT[k % 2][:, 0:kts, :], turned[fill_at[at] % 2][:, 0:kts, :])\
                  .then_inc(low_copied, 1)

            def maximum(k):
                n = (ORDER[k % SEQ_TILES] + 1) * P
                nc.vector.tensor_reduce(neg_max[:, k % RING:k % RING + 1], scores[k % 2][:, 0:n], AX.X, ALU.max,
                                        negate=True).then_inc(max_done, 1)

            def invert(pair, k):
                slot = slice(k % RING, k % RING + 1)
                dve.wait_ge(exp_done, pair * STEPS + k + 1)
                nc.vector.reciprocal(inverse[:, slot], sums[:, slot]).then_inc(inverse_done, 1)

            def divide(pair, k):
                unit, at = divmod(k % STEPS, SEQ_TILES)
                b, h = divmod(unit, 2)
                slot = slice(k % RING, k % RING + 1)
                dve.wait_ge(weighted_done, pair * STEPS + k + 1)
                dve.wait_ge(inverse_done, pair * STEPS + k + 1)
                nc.vector.tensor_scalar(attended[b][:, ORDER[at], h * HEAD_DIM:(h + 1) * HEAD_DIM], weighted[:],
                                        inverse[:, slot], None, ALU.mult).then_inc(attended_done, 1)

            def accumulate(n, b, c):
                dve.wait_ge(shared_done, n + 1)
                part = slice(b * SEQ + c * BANK, b * SEQ + (c + 1) * BANK)
                nc.vector.tensor_tensor(o1T[:, part], o1T[:, part], shared[:], ALU.add).then_inc(shared_free, 1)

            split_weights(0)
            dve.wait_ge(tables_in, 32)
            for r in range(ROTATIONS):
                part = slice(r // 2 * BANK, (r // 2 + 1) * BANK)
                dve.wait_ge(swapped_in[r % 2], (r // 2 + 1) * (P // HALF) * 16)
                nc.vector.tensor_tensor(by_sin[:], swapped[r % 2][:], sin[:, part], ALU.mult).then_inc(sin_done, 1)
                dve.wait_ge(cos_done, r + 1)
                dve.wait_ge(sin_done, r + 1)
                nc.vector.tensor_tensor(roped[r % 2][:], by_cos[r % 2][:], by_sin[:], ALU.add).then_inc(summed, 1)
                split_rotation(0, r)
            dve.wait_ge(cleared, 3)
            dve.wait_ge(scores_done, 1)
            maximum(0)

            def body(pair, first, last):
                step_uses, place, used = uses(first, last), places(first, last), used_before(pair, first)
                for k in range(STEPS):
                    if k > 2 or not first:
                        divide(pair, k - 3)
                    if k + 1 < STEPS or not last:
                        dve.wait_ge(scores_done, pair * STEPS + k + 2)
                        maximum((k + 1) % STEPS)
                    if k > 0 or not first:
                        copy_turned(pair, k - 1)
                        invert(pair, k - 1)
                    for n, (at_step, kind, arg, b) in enumerate(step_uses):
                        if at_step == k and kind == "out":
                            accumulate(used + n, b, arg)
                    ahead, at = divmod(k, PHASE)
                    if at in ROTATED_AT and not (last and ahead == BATCH - 1):
                        split_rotation(BATCH * pair + ahead + 1, ROTATED_AT[at])
                    if k == SPLIT_AT and not last:
                        dve.wait_ge(shared_done, used + place["project", PROJECTIONS - 1, 1] + 1)
                        split_weights(pair + 1)

            loop(dve, body)
            used = used_before(PAIRS - 1) + len(uses(False, True))
            divide(PAIRS, -3)
            copy_turned(PAIRS, -1)
            invert(PAIRS, -1)
            divide(PAIRS, -2)
            divide(PAIRS, -1)
            for c in range(CHUNKS):
                accumulate(used + 2 * c + 1, BATCH - 1, c)

        @block.scalar
        def _(act):
            def copy_projection(n, phase, r):
                act.wait_ge(shared_done, n + 1)
                if r > 1 or phase is not None:
                    count = (0 if phase is None else phase * ROTATIONS) + r - 1
                    act.wait_ge(cos_done, count)
                    act.wait_ge(sin_done, count)
                nc.scalar.activation(plain[r % 2][:], shared[:], ACT.Copy, scale=HEAD_DIM ** -0.5 if r % 2 else 1.0)\
                  .then_inc(shared_free, 1)

            def copy_values(n, j, b):
                act.wait_ge(shared_done, n + 1)
                tiles = slice((j - ROTATIONS) * QUARTER, (j - ROTATIONS + 1) * QUARTER)
                nc.scalar.activation(values[b][:, tiles, :], shared[:].rearrange("p (t d) -> p t d", d=P), ACT.Copy)\
                  .then_inc(shared_free, 1)

            def copy_attended(n, c):
                act.wait_ge(shared_done, n + 1)
                nc.scalar.activation(attendedT[c][:], shared[:], ACT.Copy).then_inc(shared_free, 1)

            def exponentials(pair, k):
                act.wait_ge(max_done, pair * STEPS + k + 1)
                wait_count(act, fill_done, fills_before(pair, k - RING + 1))
                n = (ORDER[k % SEQ_TILES] + 1) * P
                at = slice(k % RING, k % RING + 1)
                nc.scalar.activation(probs[k % RING][:, 0:n], scores[k % 2][:, 0:n], ACT.Exp, bias=neg_max[:, at],
                                     accum_out=sums[:, at]).then_inc(exp_done, 1)

            def copy_turned(pair, k):
                at = k % SEQ_TILES
                if fills_of[at] > 1:
                    kts = slice(QUARTER, ORDER[at] + 1)
                    act.wait_ge(fill_done, fills_before(pair, k) + 2)
                    nc.scalar.activation(probsT[k % 2][:, kts, :], turned[(fill_at[at] + 1) % 2][:, 0:ORDER[at] + 1 - QUARTER, :],
                                         ACT.Copy).then_inc(high_copied, 1)

            for j in range(PROJECTIONS):
                if j < ROTATIONS:
                    copy_projection(j, None, j)
                else:
                    copy_values(j, j, 0)
            exponentials(0, 0)

            def body(pair, first, last):
                step_uses, place, used = uses(first, last), places(first, last), used_before(pair, first)
                for k in range(STEPS):
                    if k > 0 or not first:
                        copy_turned(pair, k - 1)
                    if k + 1 < STEPS or not last:
                        exponentials(pair, k + 1)
                    for n, (at_step, kind, arg, b) in enumerate(step_uses):
                        if at_step != k:
                            continue
                        if kind == "turn":
                            copy_attended(used + n, arg)
                        elif kind == "project" and arg < ROTATIONS:
                            copy_projection(used + n, BATCH * pair + (1 if b else 2), arg)
                        elif kind == "project":
                            copy_values(used + n, arg, b)

            loop(act, body)
            used = used_before(PAIRS - 1) + len(uses(False, True))
            copy_turned(PAIRS, -1)
            for c in range(CHUNKS):
                copy_attended(used + 2 * c, c)


def project_out(nc, w_o2, gamma, o1T, x):
    with ExitStack() as stack:
        m = Memory(nc, stack, "out_")
        wo2 = m.sb("wo2", [P, DIM])
        gammas = m.sb("gammas", [P, DIM])
        stats = m.sb("stats", [P, TILES, 6])
        mean_var = m.sb("mean_var", [P, TILES, 2])
        var_eps = m.sb("var_eps", [P, TILES])
        root = m.sb("root", [P, TILES])
        rstd = m.sb("rstd", [P, TILES])
        scratch = m.sb("scratch", [P, TILES])
        y = m.sb("y", [P, TILES, DIM])
        product = [m.ps(f"product{c}", [P, BANK]) for c in range(ALL_CHUNKS)]
        loaded, chain, relu_done, product_done, var_ready, root_ready = (
            m.sem(n) for n in ("loaded", "chain", "relu_done", "product_done", "var_ready", "root_ready"))
        block = stack.enter_context(nc.Block())

        @block.sync
        def _(sync):
            sync.dma_start(wo2[:], w_o2).then_inc(loaded, 16)
            sync.dma_start(gammas[:], gamma.rearrange("(a n) -> a n", a=1).broadcast_to([P, DIM])).then_inc(loaded, 16)

        @block.tensor
        def _(pe):
            pe.wait_ge(loaded, 32)
            for t in range(TILES):
                c, i = divmod(t, BANK // P)
                pe.wait_ge(relu_done, c + 1)
                last = nc.tensor.matmul(product[c][:, i * P:(i + 1) * P], o1T[:, t * P:(t + 1) * P], wo2[:],
                                        start=True, stop=True)
                if i == BANK // P - 1:
                    last.then_inc(product_done, 1)

        @block.scalar
        def _(act):
            act.wait_ge(var_ready, 1)
            nc.scalar.activation(root[:], var_eps[:], ACT.Sqrt).then_inc(root_ready, 1)

        @block.vector
        def _(dve):
            link = counter(dve, chain)
            for c in range(ALL_CHUNKS):
                part = o1T[:, c * BANK:(c + 1) * BANK]
                nc.vector.tensor_scalar(part, part, 0.0, None, ALU.max).then_inc(relu_done, 1)

            def tile(t):
                c, i = divmod(t, BANK // P)
                return product[c][:, i * P:(i + 1) * P]

            dve.wait_ge(product_done, ALL_CHUNKS)
            row_statistics(nc, dve, link, tile, stats, mean_var, TILES)
            reciprocal_deviation(nc, dve, link, mean_var, var_eps, var_ready, root, root_ready, rstd, scratch)
            for t in range(TILES):
                last = nc.vector.tensor_scalar(y[:, t, :], tile(t), mean_var[:, t, 0:1], rstd[:, t:t + 1],
                                               ALU.subtract, ALU.mult)
            link(last)
            dve.wait_ge(loaded, 32)
            g = gammas[:].rearrange("p (a n) -> p a n", a=1).broadcast_to([P, TILES, DIM])
            link(nc.vector.tensor_tensor(y[:], y[:], g, ALU.mult))
            link(nc.vector.tensor_tensor(x[:], x[:], y[:], ALU.add))


def split_expert_weights(nc, w1, w2, w1_hi, w1_lo, w2_hi, w2_lo):
    PARTS = 4
    per = EXPERTS // PARTS
    with ExitStack() as stack:
        m = Memory(nc, stack, "split_")
        raw1 = m.sb("raw1", [P, EXPERTS, HIDDEN])
        raw2 = m.sb("raw2", [P, ALL_SLICES, DIM])
        in1 = [m.sem(f"in1_{i}") for i in range(PARTS)]
        in2 = [m.sem(f"in2_{i}") for i in range(PARTS)]
        hi_done = m.sem("hi_done")
        block = stack.enter_context(nc.Block())

        @block.sync
        def _(sync):
            for i in range(PARTS):
                e = slice(i * per, (i + 1) * per)
                sl = slice(i * per * SLICES, (i + 1) * per * SLICES)
                sync.dma_start(raw1[:, e, :], w1[e].rearrange("e d h -> d e h")).then_inc(in1[i], 16)
                sync.dma_start(raw2[:, sl, :], w2[e].rearrange("e (s h) d -> h (e s) d", h=P)).then_inc(in2[i], 16)

        @block.vector
        def _(dve):
            for i in range(PARTS):
                cols = slice(i * per * HIDDEN, (i + 1) * per * HIDDEN)
                for n, (raw, hi, lo, came) in enumerate(((raw1, w1_hi, w1_lo, in1), (raw2, w2_hi, w2_lo, in2))):
                    flat = raw[:].rearrange("p a b -> p (a b)")
                    dve.wait_ge(came[i], 16)
                    nc.vector.tensor_copy(hi[:, cols], flat[:, cols]).then_inc(hi_done, 1)
                    dve.wait_ge(hi_done, 2 * i + n + 1)
                    nc.vector.tensor_tensor(lo[:, cols], flat[:, cols], hi[:, cols].bitcast(F32), ALU.subtract)


def gate_experts(nc, wg, bg, b1, b2, xT, ident, gates_dram, b1T, sumT, name):
    with ExitStack() as stack:
        m = Memory(nc, stack, name)
        wg_sb = m.sb("wg", [P, EXPERTS])
        bg_sb = m.sb("bg", [P, EXPERTS])
        b1_rows = m.sb("b1_rows", [ALL_SLICES, P])
        b2_sb = m.sb("b2", [EXPERTS, DIM])
        logit = m.sb("logit", [P, TILES, EXPERTS])
        decay = m.sb("decay", [P, TILES, EXPERTS])
        prob = m.sb("prob", [P, TILES, EXPERTS])
        gate = m.sb("gate", [P, TILES, EXPERTS])
        gateT = m.sb("gateT", [EXPERTS, TOKENS])
        logit_ps = m.ps("logit_ps", [P, TILES, EXPERTS])
        b1_ps = m.ps("b1_ps", [P, ALL_SLICES])
        gate_ps = [m.ps(f"gate_ps{i}", [EXPERTS, BANK]) for i in range(ALL_CHUNKS)]
        bias_ps = [m.ps(f"bias_ps{i}", [P, BANK]) for i in range(2)]
        loaded, chain, logit_done, logit_read, decay_done, gate_done, turned, copied, biased, bias_copied, stored, b1_turned = (
            m.sem(n) for n in ("loaded", "chain", "logit_done", "logit_read", "decay_done", "gate_done", "turned",
                               "copied", "biased", "bias_copied", "stored", "b1_turned"))
        block = stack.enter_context(nc.Block())

        @block.sync
        def _(sync):
            sync.dma_start(wg_sb[:], wg).then_inc(loaded, 16)
            sync.dma_start(bg_sb[:], bg.rearrange("(a n) -> a n", a=1).broadcast_to([P, EXPERTS])).then_inc(loaded, 16)
            sync.dma_start(b1_rows[:], b1.rearrange("e (s h) -> (e s) h", h=P)).then_inc(loaded, 16)
            sync.dma_start(b2_sb[:], b2).then_inc(loaded, 16)
            sync.wait_ge(copied, ALL_CHUNKS)
            sync.dma_start(gates_dram, gateT[:]).then_inc(stored, 16)
            sync.wait_ge(stored, 16)

        @block.tensor
        def _(pe):
            pe.wait_ge(loaded, 64)
            for t in range(TILES):
                last = nc.tensor.matmul(logit_ps[:, t, :], xT[:, t * P:(t + 1) * P], wg_sb[:], start=True, stop=True)
            last.then_inc(logit_done, 1)
            nc.tensor.transpose(b1_ps[:], b1_rows[:], ident[0:ALL_SLICES, 0:ALL_SLICES]).then_inc(b1_turned, 1)
            pe.wait_ge(gate_done, 1)
            for t in range(TILES):
                c, i = divmod(t, BANK // P)
                last = nc.tensor.transpose(gate_ps[c][:, i * P:(i + 1) * P], gate[:, t, :], ident[:])
                if i == BANK // P - 1:
                    last.then_inc(turned, 1)
            for c in range(ALL_CHUNKS):
                pe.wait_ge(copied, c + 1)
                if c >= 2:
                    pe.wait_ge(bias_copied, c - 1)
                nc.tensor.matmul(bias_ps[c % 2][:], b2_sb[:], gateT[:, c * BANK:(c + 1) * BANK],
                                 start=True, stop=True).then_inc(biased, 1)

        @block.scalar
        def _(act):
            act.wait_ge(b1_turned, 1)
            nc.scalar.activation(b1T[:], b1_ps[:], ACT.Copy)
            act.wait_ge(logit_read, 1)
            nc.scalar.activation(decay[:], logit[:], ACT.Exp, scale=-1.0).then_inc(decay_done, 1)
            for c in range(ALL_CHUNKS):
                act.wait_ge(turned, c + 1)
                nc.scalar.activation(gateT[:, c * BANK:(c + 1) * BANK], gate_ps[c][:], ACT.Copy).then_inc(copied, 1)
            for c in range(ALL_CHUNKS):
                act.wait_ge(biased, c + 1)
                nc.scalar.activation(sumT[:, c * BANK:(c + 1) * BANK], bias_ps[c % 2][:], ACT.Copy).then_inc(bias_copied, 1)

        @block.vector
        def _(dve):
            link = counter(dve, chain)
            dve.wait_ge(logit_done, 1)
            bias = bg_sb[:].rearrange("p (a e) -> p a e", a=1).broadcast_to([P, TILES, EXPERTS])
            nc.vector.tensor_tensor(logit[:], logit_ps[:], bias, ALU.add).then_inc(logit_read, 1)
            dve.wait_ge(decay_done, 1)
            link(nc.vector.tensor_scalar(decay[:], decay[:], 1.0, None, ALU.add))
            link(nc.vector.reciprocal(prob[:], decay[:]))
            nc.vector.scalar_tensor_tensor(gate[:], logit[:], 0.0, prob[:], ALU.is_gt, ALU.mult).then_inc(gate_done, 1)


def feed_forward(nc, gates_dram, w1_hi, w1_lo, w2_hi, w2_lo, b1T, xT_hi, xT_lo, sumT, name):
    LAG, RING = 3, 4
    with ExitStack() as stack:
        m = Memory(nc, stack, name)
        gates = m.sb("gates", [P, EXPERTS, BANK])
        hidden = [m.sb(f"hidden{i}", [P, BANK]) for i in range(RING)]
        hidden_hi = [m.sb(f"hidden_hi{i}", [P, BANK], F32R) for i in range(RING)]
        hidden_lo = [m.sb(f"hidden_lo{i}", [P, BANK], F32R) for i in range(RING)]
        gated = [m.sb(f"gated{i}", [P, BANK]) for i in range(2)]
        up_ps = [m.ps(f"up{i}", [P, BANK]) for i in range(RING)]
        down_ps = [m.ps(f"down{i}", [P, BANK]) for i in range(2)]
        gates_in = [m.sem(f"gates_in{e}") for e in range(EXPERTS)]
        up_done, hi_done, relu_done, lo_done, down_done, gated_done, summed = (
            m.sem(n) for n in ("up_done", "hi_done", "relu_done", "lo_done", "down_done", "gated_done", "summed"))
        block = stack.enter_context(nc.Block())

        @block.sync
        def _(sync):
            def load_gates(chunk, e):
                rows = gates_dram[e:e + 1, bass.ds(chunk * BANK, BANK)].broadcast_to([P, BANK])
                sync.dma_start(gates[:, e, :], rows).then_inc(gates_in[e], 16)

            for e in range(EXPERTS):
                load_gates(0, e)
            with sync.Fori(0, ALL_CHUNKS - 1) as chunk:
                for e in range(EXPERTS):
                    sync.wait_ge(gated_done, chunk * EXPERTS + e + 1)
                    load_gates(chunk + 1, e)

        @block.tensor
        def _(pe):
            with pe.Fori(0, ALL_CHUNKS) as chunk:
                tokens = bass.ds(chunk * BANK, BANK)
                before = chunk * ALL_SLICES

                def up(n):
                    if n >= RING:
                        pe.wait_ge(relu_done, before + n - RING + 1)
                    w = slice(n * P, (n + 1) * P)
                    for i, (wt, xt) in enumerate(((w1_hi, xT_hi), (w1_hi, xT_lo), (w1_lo, xT_hi))):
                        last = nc.tensor.matmul(up_ps[n % RING][:], wt[:, w], xt[:, tokens], start=i == 0, stop=i == 2)
                    last.then_inc(up_done, 1)

                def down(n):
                    e, s = divmod(n, SLICES)
                    w = slice(n * P, (n + 1) * P)
                    pe.wait_ge(lo_done, before + n + 1)
                    if s == 0 and e >= 2:
                        pe.wait_ge(gated_done, chunk * EXPERTS + e - 1)
                    for i, (wt, ht) in enumerate(((w2_hi, hidden_hi), (w2_hi, hidden_lo), (w2_lo, hidden_hi))):
                        last = nc.tensor.matmul(down_ps[e % 2][:], wt[:, w], ht[n % RING][:],
                                                start=s == 0 and i == 0, stop=s == SLICES - 1 and i == 2)
                    last.then_inc(down_done, 1)

                for n in range(LAG):
                    up(n)
                for n in range(ALL_SLICES):
                    if n + LAG < ALL_SLICES:
                        up(n + LAG)
                    down(n)

        @block.scalar
        def _(act):
            with act.Fori(0, ALL_CHUNKS) as chunk:
                before = chunk * ALL_SLICES
                for n in range(ALL_SLICES):
                    act.wait_ge(up_done, before + n + 1)
                    if n >= RING:
                        act.wait_ge(down_done, before + n - RING + 1)
                    bias = b1T[:, n:n + 1]
                    nc.scalar.activation(hidden_hi[n % RING][:], up_ps[n % RING][:], ACT.Relu, bias=bias)\
                      .then_inc(hi_done, 1)
                    nc.scalar.activation(hidden[n % RING][:], up_ps[n % RING][:], ACT.Relu, bias=bias)\
                      .then_inc(relu_done, 1)

        @block.vector
        def _(dve):
            with dve.Fori(0, ALL_CHUNKS) as chunk:
                before = chunk * ALL_SLICES
                tokens = bass.ds(chunk * BANK, BANK)

                def combine(e):
                    dve.wait_ge(gates_in[e], (chunk + 1) * 16)
                    dve.wait_ge(down_done, before + (e + 1) * SLICES)
                    nc.vector.tensor_tensor(gated[e % 2][:], down_ps[e % 2][:], gates[:, e, :], ALU.mult)\
                      .then_inc(gated_done, 1)
                    dve.wait_ge(gated_done, chunk * EXPERTS + e + 1)
                    nc.vector.tensor_tensor(sumT[:, tokens], sumT[:, tokens], gated[e % 2][:], ALU.add)\
                      .then_inc(summed, 1)
                    dve.wait_ge(summed, chunk * EXPERTS + e + 1)

                for n in range(ALL_SLICES):
                    dve.wait_ge(hi_done, before + n + 1)
                    dve.wait_ge(relu_done, before + n + 1)
                    nc.vector.tensor_tensor(hidden_lo[n % RING][:], hidden[n % RING][:],
                                            hidden_hi[n % RING][:].bitcast(F32), ALU.subtract).then_inc(lo_done, 1)
                    if n >= 2 * SLICES - 1 and n % SLICES == SLICES - 1:
                        combine(n // SLICES - 1)
                combine(EXPERTS - 1)


def add_turned(nc, sumT, x, ident, name, out=None):
    with ExitStack() as stack:
        m = Memory(nc, stack, name)
        turned = [m.ps(f"turned{i}", [P, BANK]) for i in range(ALL_CHUNKS)]
        turn_done, added, stored = m.sem("turn_done"), m.sem("added"), m.sem("stored")
        block = stack.enter_context(nc.Block())
        per = BANK // P

        @block.tensor
        def _(pe):
            for t in range(TILES):
                c, i = divmod(t, per)
                last = nc.tensor.transpose(turned[c][:, i * P:(i + 1) * P], sumT[:, t * P:(t + 1) * P], ident[:])
                if i == per - 1:
                    last.then_inc(turn_done, 1)

        @block.vector
        def _(dve):
            for c in range(ALL_CHUNKS):
                dve.wait_ge(turn_done, c + 1)
                part = x[:, c * per:(c + 1) * per, :]
                nc.vector.tensor_tensor(part, part, turned[c][:].rearrange("p (t d) -> p t d", d=DIM), ALU.add)\
                  .then_inc(added, 1)

        if out is not None:
            @block.sync
            def _(sync):
                for c in range(ALL_CHUNKS):
                    sync.wait_ge(added, c + 1)
                    sync.dma_start(out[:, c * per:(c + 1) * per, :], x[:, c * per:(c + 1) * per, :]).then_inc(stored, 16)
                sync.wait_ge(stored, 16 * ALL_CHUNKS)


def full_attention(nc, qk, vo, xn, xT_hi, xT_lo, ident, x):
    QUARTER = BANK // P
    FILLS = SEQ_TILES // QUARTER
    PIECE = 2
    with ExitStack() as stack:
        m = Memory(nc, stack, "full_")
        qk_raw = m.sb("qk_raw", [P, DIM])
        qk_hi = m.sb("qk_hi", [P, DIM], F32R)
        qk_lo = m.sb("qk_lo", [P, DIM], F32R)
        vo_sb = m.sb("vo", [P, DIM])
        yT = m.sb("yT", [P, TOKENS])
        yT_hi = m.sb("yT_hi", [P, TOKENS], F32R)
        yT_lo = m.sb("yT_lo", [P, TOKENS], F32R)
        neg_max = m.sb("neg_max", [P, TILES])
        sums = m.sb("sums", [P, TILES])
        inverse = m.sb("inverse", [P, TILES])
        probs = [m.sb(f"probs{i}", [P, SEQ]) for i in range(2)]
        probsT = [m.sb(f"probsT{i}", [P, SEQ_TILES, BANK]) for i in range(2)]
        meanT = [m.sb(f"meanT{i}", [P, BANK]) for i in range(2)]
        scores = [m.ps(f"scores{i}", [P, SEQ]) for i in range(2)]
        turned = [m.ps(f"turned{i}", [P, QUARTER, P]) for i in range(2)]
        weighted = m.ps("weighted", [P, BANK])
        result = m.ps("result", [P, QUARTER, DIM])
        (loaded, qk_hi_done, qk_lo_done, y_done, y_copied, y_hi_done, y_lo_done, scores_done, max_done, exp_done,
         inverse_done, fill_done, fill_copied, weighted_done, mean_done, result_done, result_read) = (
            m.sem(n) for n in ("loaded", "qk_hi_done", "qk_lo_done", "y_done", "y_copied", "y_hi_done", "y_lo_done",
                               "scores_done", "max_done", "exp_done", "inverse_done", "fill_done", "fill_copied",
                               "weighted_done", "mean_done", "result_done", "result_read"))
        block = stack.enter_context(nc.Block())

        @block.sync
        def _(sync):
            sync.dma_start(qk_raw[:], qk).then_inc(loaded, 16)
            sync.dma_start(vo_sb[:], vo).then_inc(loaded, 16)

        @block.tensor
        def _(pe):
            pe.wait_ge(qk_lo_done, 1)
            for c in range(ALL_CHUNKS):
                part = slice(c * BANK, (c + 1) * BANK)
                into = scores[c // 2][:, (c % 2) * BANK:(c % 2 + 1) * BANK]
                for i, (wt, xt) in enumerate(((qk_hi, xT_hi), (qk_hi, xT_lo), (qk_lo, xT_hi))):
                    last = nc.tensor.matmul(into, wt[:], xt[:, part], start=i == 0, stop=i == 2)
                last.then_inc(y_done, 1)

            def score(k):
                b = k // SEQ_TILES
                cols = slice(k * P, (k + 1) * P)
                pe.wait_ge(y_lo_done, k // QUARTER + 1)
                pe.wait_ge(y_copied, 2 * (k % 2) + 2)
                if k >= 2:
                    pe.wait_ge(exp_done, k - 1)
                for c in range(CHUNKS):
                    keys = slice(b * SEQ + c * BANK, b * SEQ + (c + 1) * BANK)
                    for i, (yt, xt) in enumerate(((yT_hi, xT_hi), (yT_hi, xT_lo), (yT_lo, xT_hi))):
                        last = nc.tensor.matmul(scores[k % 2][:, c * BANK:(c + 1) * BANK], yt[:, cols], xt[:, keys],
                                                start=i == 0, stop=i == 2)
                last.then_inc(scores_done, 1)

            def turn(k):
                pe.wait_ge(exp_done, k + 1)
                for g in range(FILLS):
                    fill = k * FILLS + g
                    if fill >= 2:
                        pe.wait_ge(fill_copied, fill - 1)
                    for i in range(QUARTER):
                        kt = g * QUARTER + i
                        last = nc.tensor.transpose(turned[fill % 2][:, i, :], probs[k % 2][:, kt * P:(kt + 1) * P], ident[:])
                    last.then_inc(fill_done, 1)

            def weigh(j, piece):
                b = j // CHUNKS
                if piece == 0:
                    pe.wait_ge(fill_copied, (j + 1) * QUARTER * FILLS)
                    if j >= 1:
                        pe.wait_ge(mean_done, j)
                for kt in range(piece * PIECE, (piece + 1) * PIECE):
                    last = nc.tensor.matmul(weighted[:], xn[:, b * SEQ_TILES + kt, :], probsT[j % 2][:, kt, :],
                                            start=kt == 0, stop=kt == SEQ_TILES - 1)
                if piece == SEQ_TILES // PIECE - 1:
                    last.then_inc(weighted_done, 1)

            def multiply_out(j):
                pe.wait_ge(mean_done, j + 1)
                pe.wait_ge(loaded, 32)
                if j >= 1:
                    pe.wait_ge(result_read, j)
                for i in range(QUARTER):
                    last = nc.tensor.matmul(result[:, i, :], meanT[j % 2][:, i * P:(i + 1) * P], vo_sb[:],
                                            start=True, stop=True)
                last.then_inc(result_done, 1)

            score(0)
            for k in range(TILES + 2 * QUARTER):
                if k + 1 < TILES:
                    score(k + 1)
                if 1 <= k <= TILES:
                    turn(k - 1)
                j, piece = divmod(k - QUARTER - 1, QUARTER)
                if 0 <= j < ALL_CHUNKS:
                    weigh(j, piece)
                if piece == 1 and 0 <= j - 1 < ALL_CHUNKS:
                    multiply_out(j - 1)

        @block.vector
        def _(dve):
            dve.wait_ge(loaded, 32)
            nc.vector.tensor_copy(qk_hi[:], qk_raw[:]).then_inc(qk_hi_done, 1)
            dve.wait_ge(qk_hi_done, 1)
            nc.vector.tensor_tensor(qk_lo[:], qk_raw[:], qk_hi[:].bitcast(F32), ALU.subtract).then_inc(qk_lo_done, 1)
            for c in range(ALL_CHUNKS):
                part = slice(c * BANK, (c + 1) * BANK)
                dve.wait_ge(y_copied, c + 1)
                nc.vector.tensor_copy(yT_hi[:, part], yT[:, part]).then_inc(y_hi_done, 1)
                dve.wait_ge(y_hi_done, c + 1)
                nc.vector.tensor_tensor(yT_lo[:, part], yT[:, part], yT_hi[:, part].bitcast(F32),
                                        ALU.subtract).then_inc(y_lo_done, 1)

            def add_result(j):
                dve.wait_ge(result_done, j + 1)
                for i in range(QUARTER):
                    t = j * QUARTER + i
                    last = nc.vector.scalar_tensor_tensor(x[:, t, :], result[:, i, :], inverse[:, t:t + 1], x[:, t, :],
                                                          ALU.mult, ALU.add)
                last.then_inc(result_read, 1)

            for k in range(TILES + 2 * QUARTER):
                if k < TILES:
                    dve.wait_ge(scores_done, k + 1)
                    nc.vector.tensor_reduce(neg_max[:, k:k + 1], scores[k % 2][:], AX.X, ALU.max,
                                            negate=True).then_inc(max_done, 1)
                if 1 <= k <= TILES:
                    dve.wait_ge(exp_done, k)
                    nc.vector.reciprocal(inverse[:, k - 1:k], sums[:, k - 1:k]).then_inc(inverse_done, 1)
                j, piece = divmod(k - QUARTER - 1, QUARTER)
                if piece == 1 and 0 <= j - 1 < ALL_CHUNKS:
                    dve.wait_ge(inverse_done, j * QUARTER)
                    add_result(j - 1)

        @block.scalar
        def _(act):
            for c in range(ALL_CHUNKS):
                act.wait_ge(y_done, c + 1)
                nc.scalar.activation(yT[:, c * BANK:(c + 1) * BANK], scores[c // 2][:, (c % 2) * BANK:(c % 2 + 1) * BANK],
                                     ACT.Copy, scale=float(DIM) ** -0.5).then_inc(y_copied, 1)
            for k in range(TILES + 2 * QUARTER):
                if k < TILES:
                    act.wait_ge(max_done, k + 1)
                    nc.scalar.activation(probs[k % 2][:], scores[k % 2][:], ACT.Exp, bias=neg_max[:, k:k + 1],
                                         accum_out=sums[:, k:k + 1]).then_inc(exp_done, 1)
                if 1 <= k <= TILES:
                    j, t = divmod(k - 1, QUARTER)
                    if t == 0 and j >= 2:
                        act.wait_ge(weighted_done, j - 1)
                    for g in range(FILLS):
                        fill = (k - 1) * FILLS + g
                        act.wait_ge(fill_done, fill + 1)
                        nc.scalar.activation(probsT[j % 2][:, g * QUARTER:(g + 1) * QUARTER, t * P:(t + 1) * P],
                                             turned[fill % 2][:], ACT.Copy).then_inc(fill_copied, 1)
                j, piece = divmod(k - QUARTER - 1, QUARTER)
                if piece == QUARTER - 1 and 0 <= j < ALL_CHUNKS:
                    act.wait_ge(weighted_done, j + 1)
                    nc.scalar.activation(meanT[j % 2][:], weighted[:], ACT.Copy).then_inc(mean_done, 1)


def hybrid_layer(nc, x_dram, w_qkv, w_o1, w_o2, gamma, qk, vo, wg, bg, w1, b1, w2, b2, cos_table, sin_table, out, stop=9):
    x_rows = x_dram.rearrange("b (t p) d -> p (b t) d", p=P)
    out_rows = out.rearrange("b (t p) d -> p (b t) d", p=P)
    gates_dram = nc.dram_tensor("gates", (EXPERTS, TOKENS), F32, kind="Internal").ap()
    with ExitStack() as stack:
        m = Memory(nc, stack)
        ident = m.sb("ident", [P, P])
        x = m.sb("x", [P, TILES, DIM])
        xT_hi = m.sb("xT_hi", [P, TOKENS], F32R)
        xT_lo = m.sb("xT_lo", [P, TOKENS], F32R)
        sumT = m.sb("sumT", [P, TOKENS])
        ident_done, stored = m.sem("ident_done"), m.sem("stored")

        def normalise(name, load=None):
            normalise_and_transpose(nc, x, xn, xT, xT_hi, xT_lo, ident, name, load)

        def store():
            with nc.Block() as block:
                @block.sync
                def _(sync):
                    sync.dma_start(out_rows, x[:]).then_inc(stored, 16)
                    sync.wait_ge(stored, 16)

        def load_x(sync, loaded):
            sync.dma_start(x[:], x_rows).then_inc(loaded, 16)
            return 16

        with nc.Block() as block:
            @block.gpsimd
            def _(pool):
                nc.gpsimd.memset(ident[:], 0.0).then_inc(ident_done, 1)
                pool.wait_ge(ident_done, 1)
                nc.gpsimd.affine_select(out=ident[:], in_=ident[:], compare_op=ALU.not_equal, fill=1.0, base=0,
                                        pattern=[[-1, P]], channel_multiplier=1)

        with ExitStack() as early:
            e = Memory(nc, early, "early_")
            normalise_and_transpose(nc, x, e.sb("xn", [P, TILES, DIM]), e.sb("xT", [P, TOKENS]), xT_hi, xT_lo, ident,
                                    "ln1_", load_x)
        causal_attention(nc, w_qkv, w_o1, cos_table, sin_table, xT_hi, xT_lo, ident, sumT)
        project_out(nc, w_o2, gamma, sumT, x)
        if stop == 1:
            return store()
        xn = m.sb("xn", [P, TILES, DIM])
        xT = m.sb("xT", [P, TOKENS])
        w1_hi = m.sb("w1_hi", [P, EXPERTS * HIDDEN], F32R)
        w1_lo = m.sb("w1_lo", [P, EXPERTS * HIDDEN], F32R)
        w2_hi = m.sb("w2_hi", [P, ALL_SLICES * DIM], F32R)
        w2_lo = m.sb("w2_lo", [P, ALL_SLICES * DIM], F32R)
        b1T = m.sb("b1T", [P, ALL_SLICES])

        def feed(name, out=None):
            gate_experts(nc, wg, bg, b1, b2, xT, ident, gates_dram, b1T, sumT, name + "gate_")
            feed_forward(nc, gates_dram, w1_hi, w1_lo, w2_hi, w2_lo, b1T, xT_hi, xT_lo, sumT, name)
            add_turned(nc, sumT, x, ident, name + "add_", out)

        split_expert_weights(nc, w1, w2, w1_hi, w1_lo, w2_hi, w2_lo)
        normalise("ln2_")
        feed("ff1_")
        if stop == 2:
            return store()
        normalise("ln3_")
        full_attention(nc, qk, vo, xn, xT_hi, xT_lo, ident, x)
        if stop == 3:
            return store()
        normalise("ln4_")
        feed("ff2_", out_rows)


_INS = ['L0_attn_a_x', 'L0_attn_a_W_qkv', 'L0_attn_a_W_o1', 'L0_attn_a_W_o2', 'L0_attn_a_gamma', 'L0_attn_b_QK',
        'L0_attn_b_VO', 'L0_ffn_Wg', 'L0_ffn_bg', 'L0_ffn_W1', 'L0_ffn_b1', 'L0_ffn_W2', 'L0_ffn_b2']


def rotation_tables():
    inv_freq = (np.float32(1.0) / np.power(np.float32(10000.0),
                np.arange(0, HEAD_DIM, 2, dtype=np.float32) / np.float32(HEAD_DIM))).astype(np.float32)
    angle = inv_freq[:, None] * np.arange(SEQ, dtype=np.float32)[None, :]
    cos, sin = np.cos(angle), np.sin(angle)
    return np.concatenate([cos] * 4, 0), np.concatenate([-sin, sin] * 2, 0)


def kernel(**inputs):
    import concourse.bacc as bacc
    from concourse.bass_utils import run_bass_kernel_spmd

    nc = bacc.Bacc("TRN2", target_bir_lowering=False, num_devices=1)
    arrays, args = {}, []
    cos, sin = rotation_tables()
    for name, a in [(n, inputs[n]) for n in _INS] + [("cos_table", cos), ("sin_table", sin)]:
        a = np.ascontiguousarray(a)
        arrays[f"in_{name}"] = a
        args.append(nc.dram_tensor(f"in_{name}", a.shape, mybir.dt.from_np(a.dtype), kind="ExternalInput").ap())
    out = nc.dram_tensor("out_0", (BATCH, SEQ, DIM), F32, kind="ExternalOutput").ap()
    hybrid_layer(nc, *args, out)
    r = run_bass_kernel_spmd(nc, [arrays], core_ids=[0])
    return r.results[0]["out_0"]
```

```python
import numpy as np
import concourse.bass as bass
from concourse import mybir
from contextlib import ExitStack

F32 = mybir.dt.float32
F32R = mybir.dt.float32r
ALU = mybir.AluOpType
ACT = mybir.ActivationFunctionType
AX = mybir.AxisListType

P = 128
BANK = 512
BATCH, SEQ, DIM = 2, 1024, 128
TOKENS = BATCH * SEQ
TILES = TOKENS // P
SEQ_TILES = SEQ // P
CHUNKS = SEQ // BANK
ALL_CHUNKS = TOKENS // BANK
HEADS, HEAD_DIM = 16, 64
INNER = HEADS * HEAD_DIM
PAIRS = HEADS // 2
EXPERTS, HIDDEN = 8, 512
SLICES = HIDDEN // P
ALL_SLICES = EXPERTS * SLICES
EPS = 1e-5
MASKED = -1e30


def counter(engine, sem):
    count = [0]

    def link(instruction):
        count[0] += 1
        instruction.then_inc(sem, 1)
        engine.wait_ge(sem, count[0])

    return link


def held(engine, value):
    return value if isinstance(value, int) else engine.snap(value)


def wait_count(engine, sem, count):
    if not isinstance(count, int) or count > 0:
        engine.wait_ge(sem, count)


class Memory:

    def __init__(self, nc, stack, prefix=""):
        self.nc, self.stack, self.prefix = nc, stack, prefix

    def sb(self, name, shape, dtype=F32):
        return self.stack.enter_context(self.nc.sbuf_tensor(self.prefix + name, shape, dtype))

    def ps(self, name, shape, dtype=F32):
        return self.stack.enter_context(self.nc.psum_tensor(self.prefix + name, shape, dtype))

    def sem(self, name):
        return self.stack.enter_context(self.nc.semaphore(self.prefix + name))


def reciprocal_deviation(nc, dve, link, mean_var, var_eps, var_ready, root, root_ready, rstd, scratch):
    nc.vector.tensor_scalar(var_eps[:], mean_var[:, :, 1], EPS, None, ALU.add).then_inc(var_ready, 1)
    dve.wait_ge(root_ready, 1)
    link(nc.vector.reciprocal(rstd[:], root[:]))
    link(nc.vector.tensor_tensor(scratch[:], rstd[:], rstd[:], ALU.mult))
    link(nc.vector.tensor_tensor(scratch[:], scratch[:], var_eps[:], ALU.mult))
    link(nc.vector.tensor_scalar(scratch[:], scratch[:], -0.5, 1.5, ALU.mult, ALU.add))
    link(nc.vector.tensor_tensor(rstd[:], rstd[:], scratch[:], ALU.mult))


class GateInputs:

    def __init__(self, m):
        self.wg = m.sb("wg", [P, EXPERTS])
        self.bg = m.sb("bg", [P, EXPERTS])
        self.b1_rows = m.sb("b1_rows", [ALL_SLICES, P])
        self.b2_rows = m.sb("b2_rows", [EXPERTS, DIM])
        self.b1T = m.sb("b1T", [P, ALL_SLICES])
        self.b2T = m.sb("b2T", [P, EXPERTS])
        self.loaded = m.sem("gate_inputs_loaded")
        self.stored = m.sem("gates_stored")

    def load(self, sync, wg, bg, b1, b2):
        sync.dma_start(self.wg[:], wg).then_inc(self.loaded, 16)
        sync.dma_start(self.bg[:], bg.rearrange("(a n) -> a n", a=1).broadcast_to([P, EXPERTS])).then_inc(self.loaded, 16)
        sync.dma_start(self.b1_rows[:], b1.rearrange("e (s h) -> (e s) h", h=P)).then_inc(self.loaded, 16)
        sync.dma_start(self.b2_rows[:], b2).then_inc(self.loaded, 16)


def normalise_and_transpose(nc, x, xn, xT, xT_hi, xT_lo, ident, name, load=None, addT=None, gate=None,
                            gates_dram=None, split=None, copy=None):
    QUARTER = BANK // P
    OWN = 11
    with ExitStack() as stack:
        m = Memory(nc, stack, name)
        stats = m.sb("stats", [P, TILES, 6])
        mean_var = m.sb("mean_var", [P, TILES, 2])
        var_eps = m.sb("var_eps", [P, TILES])
        root = m.sb("root", [P, TILES])
        rstd = m.sb("rstd", [P, TILES])
        shift = m.sb("shift", [P, TILES])
        scratch = m.sb("scratch", [P, TILES])
        turned = [m.ps(f"turned{i}", [P, BANK]) for i in range(ALL_CHUNKS)]
        loaded = [m.sem(f"loaded{c}") for c in range(ALL_CHUNKS)] if load is not None else None
        chain, var_ready, root_ready, shift_ready, own_ready, other_ready, turned_ready, xT_ready, hi_ready = (
            m.sem(n) for n in ("chain", "var_ready", "root_ready", "shift_ready", "own_ready", "other_ready",
                               "turned_ready", "xT_ready", "hi_ready"))
        if addT is not None:
            add_turned, added = m.sem("add_turned"), m.sem("added")
        if gate is not None:
            logit = m.sb("logit", [P, TILES, EXPERTS])
            decay = m.sb("decay", [P, TILES, EXPERTS])
            prob = m.sb("prob", [P, TILES, EXPERTS])
            gates = m.sb("gates", [P, TILES, EXPERTS])
            gateT = m.sb("gateT", [EXPERTS, TOKENS])
            logit_ps = m.ps("logit_ps", [P, TILES, EXPERTS])
            b1_ps = m.ps("b1_ps", [P, ALL_SLICES])
            b2_ps = m.ps("b2_ps", [P, EXPERTS])
            logit_done, logit_read, decay_done, gate_done, gate_turned, gate_copied, b_turned = (
                m.sem(n) for n in ("logit_done", "logit_read", "decay_done", "gate_done", "gate_turned", "gate_copied",
                                   "b_turned"))
        block = stack.enter_context(nc.Block())

        if load is not None or gate is not None:
            @block.sync
            def _(sync):
                if load is not None:
                    load(sync, loaded)
                if gate is not None:
                    sync.wait_ge(gate_copied, ALL_CHUNKS)
                    sync.dma_start(gates_dram, gateT[:]).then_inc(gate.stored, 16)

        if split is not None:
            @block.gpsimd
            def _(pool):
                split(pool)

        @block.vector
        def _(dve):
            link = counter(dve, chain)
            for c in range(ALL_CHUNKS):
                tiles = slice(c * QUARTER, (c + 1) * QUARTER)
                if load is not None:
                    dve.wait_ge(loaded[c], 16)
                if addT is not None:
                    dve.wait_ge(add_turned, c + 1)
                    nc.vector.tensor_tensor(x[:, tiles, :], x[:, tiles, :], turned[c][:].rearrange("p (t d) -> p t d", d=DIM),
                                            ALU.add).then_inc(added, 1)
                    dve.wait_ge(added, c + 1)
                for t in range(c * QUARTER, (c + 1) * QUARTER):
                    last = nc.vector.bn_stats(stats[:, t, :], x[:, t, :])
            link(last)
            for t in range(TILES):
                last = nc.vector.bn_aggr(mean_var[:, t, :], stats[:, t, :])
            link(last)
            reciprocal_deviation(nc, dve, link, mean_var, var_eps, var_ready, root, root_ready, rstd, scratch)
            nc.vector.scalar_tensor_tensor(shift[:], mean_var[:, :, 0], -1.0, rstd[:], ALU.mult, ALU.mult)\
              .then_inc(shift_ready, 1)
            for t in range(OWN):
                nc.vector.tensor_scalar(xn[:, t, :], x[:, t, :], mean_var[:, t, 0:1], rstd[:, t:t + 1],
                                        ALU.subtract, ALU.mult).then_inc(own_ready, 1)
            for c in range(ALL_CHUNKS):
                part = slice(c * BANK, (c + 1) * BANK)
                dve.wait_ge(xT_ready, c + 1)
                nc.vector.tensor_copy(xT_hi[:, part], xT[:, part]).then_inc(hi_ready, 1)
                dve.wait_ge(hi_ready, c + 1)
                nc.vector.tensor_tensor(xT_lo[:, part], xT[:, part], xT_hi[:, part].bitcast(F32), ALU.subtract)
            if gate is not None:
                dve.wait_ge(logit_done, 1)
                bias = gate.bg[:].rearrange("p (a e) -> p a e", a=1).broadcast_to([P, TILES, EXPERTS])
                nc.vector.tensor_tensor(logit[:], logit_ps[:], bias, ALU.add).then_inc(logit_read, 1)
                dve.wait_ge(decay_done, 1)
                link(nc.vector.tensor_scalar(decay[:], decay[:], 1.0, None, ALU.add))
                link(nc.vector.reciprocal(prob[:], decay[:]))
                nc.vector.scalar_tensor_tensor(gates[:], logit[:], 0.0, prob[:], ALU.is_gt, ALU.mult).then_inc(gate_done, 1)

        @block.tensor
        def _(pe):
            if addT is not None:
                for t in range(TILES):
                    c, i = divmod(t, QUARTER)
                    turn = nc.tensor.transpose(turned[c][:, i * P:(i + 1) * P], addT[:, t * P:(t + 1) * P], ident[:])
                    if i == QUARTER - 1:
                        turn.then_inc(add_turned, 1)
            if gate is not None:
                pe.wait_ge(gate.loaded, 64)
                nc.tensor.transpose(b1_ps[:], gate.b1_rows[:], ident[0:ALL_SLICES, 0:ALL_SLICES])
                nc.tensor.transpose(b2_ps[:], gate.b2_rows[:], ident[0:EXPERTS, 0:EXPERTS]).then_inc(b_turned, 1)
            for t in range(TILES):
                if t < OWN:
                    pe.wait_ge(own_ready, t + 1)
                else:
                    pe.wait_ge(other_ready, t - OWN + 1)
                c, i = divmod(t, QUARTER)
                turn = nc.tensor.transpose(turned[c][:, i * P:(i + 1) * P], xn[:, t, :], ident[:])
                if i == QUARTER - 1:
                    turn.then_inc(turned_ready, 1)
            if gate is not None:
                for t in range(TILES):
                    if t % QUARTER == 0:
                        pe.wait_ge(xT_ready, t // QUARTER + 1)
                    last = nc.tensor.matmul(logit_ps[:, t, :], xT[:, t * P:(t + 1) * P], gate.wg[:], start=True, stop=True)
                last.then_inc(logit_done, 1)
                pe.wait_ge(gate_done, 1)
                for t in range(TILES):
                    c, i = divmod(t, QUARTER)
                    last = nc.tensor.transpose(turned[c][0:EXPERTS, i * P:(i + 1) * P], gates[:, t, :], ident[:])
                    if i == QUARTER - 1:
                        last.then_inc(gate_turned, 1)

        @block.scalar
        def _(act):
            if gate is not None:
                act.wait_ge(b_turned, 1)
                nc.scalar.activation(gate.b1T[:], b1_ps[:], ACT.Copy)
                nc.scalar.activation(gate.b2T[:], b2_ps[:], ACT.Copy)
            if copy is not None:
                copy(act)
            act.wait_ge(var_ready, 1)
            nc.scalar.activation(root[:], var_eps[:], ACT.Sqrt).then_inc(root_ready, 1)
            act.wait_ge(shift_ready, 1)
            for t in range(OWN, TILES):
                nc.scalar.activation(xn[:, t, :], x[:, t, :], ACT.Identity, bias=shift[:, t:t + 1],
                                     scale=rstd[:, t:t + 1]).then_inc(other_ready, 1)
            for c in range(ALL_CHUNKS):
                act.wait_ge(turned_ready, c + 1)
                nc.scalar.activation(xT[:, c * BANK:(c + 1) * BANK], turned[c][:], ACT.Copy).then_inc(xT_ready, 1)
            if gate is not None:
                act.wait_ge(logit_read, 1)
                nc.scalar.activation(decay[:], logit[:], ACT.Exp, scale=-1.0).then_inc(decay_done, 1)
                for c in range(ALL_CHUNKS):
                    act.wait_ge(gate_turned, c + 1)
                    nc.scalar.activation(gateT[:, c * BANK:(c + 1) * BANK], turned[c][0:EXPERTS, :], ACT.Copy)\
                      .then_inc(gate_copied, 1)


def causal_attention(nc, w_qkv, w_o1, cos, sin, tables_in, raw, w_in, load_weights, xT_hi, xT_lo, ident, o1T, load_later, split_later):
    UNITS = BATCH * 2
    PHASE = 2 * SEQ_TILES
    STEPS = BATCH * PHASE
    QUARTER = BANK // P
    RING = 4
    ORDER = (0, 1, 4, 2, 5, 3, 6, 7)
    CHUNK_AT = (ORDER.index(QUARTER - 1) + 1, SEQ_TILES)
    FIRST_LONG = next(at for at, i in enumerate(ORDER) if i >= QUARTER)
    fills_of = [i // QUARTER + 1 for i in ORDER]
    fills = [(at, g) for at in range(SEQ_TILES) for g in range(fills_of[at])]
    FILLS = len(fills)
    LONG = FILLS - SEQ_TILES
    fill_at = [sum(fills_of[:i]) for i in range(SEQ_TILES + 1)]
    long_at = [fill_at[i] - i for i in range(SEQ_TILES + 1)]
    ROTATIONS = 4
    PROJECTIONS = ROTATIONS + 2
    SHARED_AT = {0: ("project", 0), 1: ("turn", 0), 2: ("project", 1), 3: ("out", 0), 4: ("turn", 1),
                 5: ("project", 2), 6: ("out", 1), 7: ("project", 3), 9: ("project", 4), 11: ("project", 5)}
    ROTATED_AT = {4: 0, 7: 1, 9: 2, 12: 3}
    SPLIT_AT = 12
    HALF = HEAD_DIM // 2

    def uses(first, last):
        out = []
        for k in range(STEPS):
            b, at = divmod(k, PHASE)
            if at in SHARED_AT:
                kind, arg = SHARED_AT[at]
                if kind == "project" and not (last and b == BATCH - 1):
                    out.append((k, kind, arg, (b + 1) % BATCH))
                if kind != "project" and not (first and b == 0):
                    out.append((k, kind, arg, (b - 1) % BATCH))
        return out

    BODY_USES = len(uses(False, False))

    def used_before(pair, first=False):
        return PROJECTIONS if first else PROJECTIONS + len(uses(True, False)) + (pair - 1) * BODY_USES

    def places(first, last):
        return {use[1:]: n for n, use in enumerate(uses(first, last))}

    with ExitStack() as stack:
        m = Memory(nc, stack, "attn_")
        w_hi = m.sb("w_hi", [P, 3, P], F32R)
        w_lo = m.sb("w_lo", [P, 3, P], F32R)
        wo1 = m.sb("wo1", [P, DIM])
        plain = [m.sb(f"plain{i}", [P, BANK]) for i in range(2)]
        swapped = [m.sb(f"swapped{i}", [P, BANK]) for i in range(2)]
        rotated = [m.sb(f"rotated{i}", [P, BANK]) for i in range(2)]
        by_sin = m.sb("by_sin", [P, BANK])
        halves = [m.sb(f"halves{i}", [P, 2, BANK], F32R) for i in range(2)]
        q_stack = [[m.sb(f"q_stack{b}{h}", [P, SEQ], F32R) for h in range(2)] for b in range(BATCH)]
        k_stack = [[m.sb(f"k_stack{b}{h}", [P, 2, SEQ], F32R) for h in range(2)] for b in range(BATCH)]
        values = [m.sb(f"values{b}", [P, SEQ_TILES, P]) for b in range(BATCH)]
        neg_max = m.sb("neg_max", [P, RING])
        sums = m.sb("sums", [P, RING])
        inverse = m.sb("inverse", [P, RING])
        probs = [m.sb(f"probs{i}", [P, (max(ORDER[i::RING]) + 1) * P]) for i in range(RING)]
        probsT = [m.sb(f"probsT{i}", [P, SEQ_TILES, P]) for i in range(2)]
        attended = [m.sb(f"attended{b}", [P, SEQ_TILES, P]) for b in range(BATCH)]
        attendedT = [m.sb(f"attendedT{c}", [P, BANK]) for c in range(CHUNKS)]
        mask = m.sb("mask", [P, P])

        scores = [m.ps(f"scores{i}", [P, SEQ]) for i in range(2)]
        turned = [m.ps(f"turned{i}", [P, QUARTER, P]) for i in range(2)]
        weighted = m.ps("weighted", [P, HEAD_DIM])
        shared = m.ps("shared", [P, BANK])

        wo1_in, masks, cleared = m.sem("wo1_in"), m.sem("masks"), m.sem("cleared")
        w_hi_done, w_lo_done = m.sem("w_hi_done"), m.sem("w_lo_done")
        shared_done, shared_free = m.sem("shared_done"), m.sem("shared_free")
        swapped_in = [m.sem(f"swapped_in{i}") for i in range(2)]
        cos_done, sin_done, summed, hi_done, lo_done = (
            m.sem(n) for n in ("cos_done", "sin_done", "summed", "hi_done", "lo_done"))
        k_in, q_in = m.sem("k_in"), m.sem("q_in")
        scores_done, masked, max_done, exp_done, inverse_done = (
            m.sem(n) for n in ("scores_done", "masked", "max_done", "exp_done", "inverse_done"))
        fill_done, low_copied, high_copied, weighted_done, attended_done = (
            m.sem(n) for n in ("fill_done", "low_copied", "high_copied", "weighted_done", "attended_done"))

        def loop(engine, body):
            body(0, True, False)
            with engine.Fori(1, PAIRS - 1) as pair:
                body(pair, False, False)
            body(PAIRS - 1, False, True)

        def low_copies(pair, k):
            return pair * STEPS + k + 1

        def high_copies(pair, k):
            unit, at = divmod(k, SEQ_TILES)
            return pair * UNITS * LONG + unit * LONG + long_at[at + 1]

        def fills_before(pair, k):
            unit, at = divmod(k, SEQ_TILES)
            return pair * UNITS * FILLS + unit * FILLS + fill_at[at]

        block = stack.enter_context(nc.Block())

        @block.sync
        def _(sync):
            def swap(phase, r, used):
                copied = held(sync, used + 1)
                again = r > 1 or phase is not None
                multiplied = held(sync, (0 if phase is None else phase * ROTATIONS) + r - 1) if again else None
                sync.wait_ge(shared_free, copied)
                if again:
                    sync.wait_ge(sin_done, multiplied)
                for j in range(P // HALF):
                    sync.dma_start(swapped[r % 2][j * HALF:(j + 1) * HALF, :],
                                   plain[r % 2][(j ^ 1) * HALF:((j ^ 1) + 1) * HALF, :]).then_inc(swapped_in[r % 2], 16)

            def stack_rotation(phase, r, b):
                c, is_q = divmod(r, 2)
                sync.wait_ge(lo_done, phase * ROTATIONS + r + 1)
                cols = slice(c * BANK, (c + 1) * BANK)
                for h in range(2):
                    rows = slice(h * HEAD_DIM, (h + 1) * HEAD_DIM)
                    for s in range(2):
                        half = slice(s * HEAD_DIM, (s + 1) * HEAD_DIM)
                        if is_q:
                            sync.dma_start(q_stack[b][h][half, cols].bitcast(F32),
                                           halves[r % 2][rows, s, :].bitcast(F32)).then_inc(q_in, 16)
                        else:
                            sync.dma_start(k_stack[b][h][half, :, cols].bitcast(F32),
                                           halves[r % 2][rows, :, :].bitcast(F32)).then_inc(k_in, 16)

            def move_phase(phase, b, used):
                started = None if isinstance(phase, int) and phase == 0 else phase
                swap(started, 0, used[0])
                for r in range(ROTATIONS):
                    if r + 1 < ROTATIONS:
                        swap(started, r + 1, used[r + 1])
                    stack_rotation(phase, r, b)

            move_phase(0, 0, list(range(ROTATIONS)))
            load_later(sync)

            def body(pair, first, last):
                place, used = places(first, last), used_before(pair, first)
                sync.wait_ge(w_lo_done, pair + 1)
                if not last:
                    load_weights(sync, pair + 1)
                move_phase(BATCH * pair + 1, 1, [used + place["project", r, 1] for r in range(ROTATIONS)])
                if not first:
                    sync.wait_ge(shared_done, used + place["out", 1, 1] + 1)
                sync.dma_start(wo1[:], w_o1[bass.ds(pair * P, P), :]).then_inc(wo1_in, 16)
                if not last:
                    move_phase(BATCH * pair + 2, 0, [used + place["project", r, 0] for r in range(ROTATIONS)])

            loop(sync, body)

        @block.gpsimd
        def _(pool):
            nc.gpsimd.memset(mask[:], 0.0).then_inc(cleared, 1)
            nc.gpsimd.memset(o1T[:], 0.0).then_inc(cleared, 1)
            pool.wait_ge(cleared, 2)
            nc.gpsimd.affine_select(out=mask[:], in_=mask[:], compare_op=ALU.is_ge, fill=MASKED, base=0,
                                    pattern=[[-1, P]], channel_multiplier=1).then_inc(masks, 1)

            def rope_phase(phase, used):
                for r in range(ROTATIONS):
                    n = phase * ROTATIONS + r
                    part = slice(r // 2 * BANK, (r // 2 + 1) * BANK)
                    pool.wait_ge(shared_free, used[r] + 1)
                    if not (isinstance(phase, int) and phase == 0 and r < 2):
                        pool.wait_ge(lo_done, n - 1)
                    nc.gpsimd.tensor_tensor(rotated[r % 2][:], plain[r % 2][:], cos[:, part], ALU.mult)\
                      .then_inc(cos_done, 1)
                    if isinstance(phase, int) and phase == 0:
                        continue
                    pool.wait_ge(swapped_in[r % 2], (phase * 2 + r // 2 + 1) * (P // HALF) * 16)
                    pool.wait_ge(summed, n)
                    nc.gpsimd.tensor_tensor(by_sin[:], swapped[r % 2][:], sin[:, part], ALU.mult).then_inc(sin_done, 1)
                    pool.wait_ge(cos_done, n + 1)
                    pool.wait_ge(sin_done, n + 1)
                    pool.wait_ge(q_in if r % 2 else k_in, (phase * 2 + r // 2) * 4 * 16)
                    nc.gpsimd.tensor_tensor(halves[r % 2][:, 0, :], rotated[r % 2][:], by_sin[:], ALU.add)\
                      .then_inc(hi_done, 1)
                    nc.gpsimd.tensor_tensor(rotated[r % 2][:], rotated[r % 2][:], by_sin[:], ALU.add).then_inc(summed, 1)

            pool.wait_ge(tables_in, 32)
            rope_phase(0, list(range(ROTATIONS)))
            pool.wait_ge(summed, ROTATIONS)

            def body(pair, first, last):
                place, used = places(first, last), used_before(pair, first)
                rope_phase(BATCH * pair + 1, [used + place["project", r, 1] for r in range(ROTATIONS)])
                if not last:
                    rope_phase(BATCH * pair + 2, [used + place["project", r, 0] for r in range(ROTATIONS)])

            loop(pool, body)
            split_later(pool)

        @block.tensor
        def _(pe):
            def take_shared(n, first=False):
                if not first:
                    pe.wait_ge(shared_free, n)

            def project(j, b):
                if j < ROTATIONS:
                    c, is_q = divmod(j, 2)
                    w = 0 if is_q else 1
                    cols = slice(b * SEQ + c * BANK, b * SEQ + (c + 1) * BANK)
                    for n, (wt, xt) in enumerate(((w_hi, xT_hi), (w_hi, xT_lo), (w_lo, xT_hi))):
                        last = nc.tensor.matmul(shared[:], wt[:, w, :], xt[:, cols], start=n == 0, stop=n == 2)
                    last.then_inc(shared_done, 1)
                else:
                    for i in range(QUARTER):
                        t = (j - ROTATIONS) * QUARTER + i
                        cols = slice(b * SEQ + t * P, b * SEQ + (t + 1) * P)
                        for n, (xt, wt) in enumerate(((xT_hi, w_hi), (xT_hi, w_lo), (xT_lo, w_hi))):
                            last = nc.tensor.matmul(shared[:, i * P:(i + 1) * P], xt[:, cols], wt[:, 2, :],
                                                    start=n == 0, stop=n == 2)
                    last.then_inc(shared_done, 1)

            def turn_attended(pair, n, b, c):
                take_shared(n)
                pe.wait_ge(attended_done, pair * STEPS + b * PHASE + SEQ_TILES + CHUNK_AT[c])
                for i in range(QUARTER):
                    last = nc.tensor.transpose(shared[:, i * P:(i + 1) * P], attended[b][:, c * QUARTER + i, :], ident[:])
                last.then_inc(shared_done, 1)

            def multiply_out(pair, n, c):
                take_shared(n)
                pe.wait_ge(wo1_in, 16 * (pair + 1))
                nc.tensor.matmul(shared[:], wo1[:], attendedT[c][:], start=True, stop=True).then_inc(shared_done, 1)

            def score(k):
                unit, at = divmod(k, SEQ_TILES)
                i = ORDER[at]
                b, h = divmod(unit, 2)
                cols = slice(i * P, (i + 1) * P)
                into = scores[k % 2]
                for c in range(i // QUARTER + 1):
                    keys = slice(c * BANK, min((c + 1) * BANK, (i + 1) * P))
                    nc.tensor.matmul(into[:, keys], q_stack[b][h][:, cols], k_stack[b][h][:, 0, keys], start=True, stop=False)
                    last = nc.tensor.matmul(into[:, keys], q_stack[b][h][:, cols], k_stack[b][h][:, 1, keys], start=False,
                                            stop=True)
                last.then_inc(scores_done, 1)

            def turn(pair, k):
                unit, at = divmod(k, SEQ_TILES)
                for g in range(fills_of[at]):
                    back, place = divmod(fill_at[at] + g - 2, FILLS)
                    old_at, old_g = fills[place]
                    old = (unit + back) * SEQ_TILES + old_at
                    if old_g:
                        wait_count(pe, high_copied, high_copies(pair, old))
                    else:
                        wait_count(pe, low_copied, low_copies(pair, old))
                    for kt in range(QUARTER * g, min(QUARTER * (g + 1), ORDER[at] + 1)):
                        last = nc.tensor.transpose(turned[(fill_at[at] + g) % 2][:, kt - QUARTER * g, :],
                                                   probs[k % RING][:, kt * P:(kt + 1) * P], ident[:])
                    last.then_inc(fill_done, 1)

            def weigh(pair, k, values_copied=None):
                unit, at = divmod(k, SEQ_TILES)
                b, h = divmod(unit % UNITS, 2)
                if values_copied is not None:
                    pe.wait_ge(shared_free, values_copied)
                wait_count(pe, attended_done, pair * STEPS + k)
                pe.wait_ge(low_copied, low_copies(pair, k))
                for kt in range(ORDER[at] + 1):
                    if kt == QUARTER:
                        pe.wait_ge(high_copied, high_copies(pair, k))
                    last = nc.tensor.matmul(weighted[:], probsT[k % 2][:, kt, :],
                                            values[b][:, kt, h * HEAD_DIM:(h + 1) * HEAD_DIM],
                                            start=kt == 0, stop=kt == ORDER[at])
                last.then_inc(weighted_done, 1)

            pe.wait_ge(w_lo_done, 1)
            for j in range(PROJECTIONS):
                take_shared(j, j == 0)
                project(j, 0)
            pe.wait_ge(k_in, 4 * 16)
            pe.wait_ge(q_in, 4 * 16)
            score(0)

            def body(pair, first, last):
                step_uses, place, used = uses(first, last), places(first, last), used_before(pair, first)
                for k in range(STEPS):
                    if k > 0 or not first:
                        pe.wait_ge(exp_done, pair * STEPS + k)
                    if k + 1 < STEPS or not last:
                        chunk = {0: 0, FIRST_LONG: 1}.get((k + 1) % PHASE)
                        if chunk is not None:
                            stacked = ((BATCH * pair + (k + 1) // PHASE) * 2 + chunk + 1) * 4 * 16
                            pe.wait_ge(k_in, stacked)
                            pe.wait_ge(q_in, stacked)
                        score((k + 1) % STEPS)
                    if k > 0 or not first:
                        turn(pair, k - 1)
                    if k > 1 or not first:
                        if k - 2 == 0 and first:
                            copied = PROJECTIONS
                        elif k - 2 == 0:
                            copied = used - BODY_USES + places(False, False)["project", PROJECTIONS - 1, 0] + 1
                        elif k - 2 == PHASE:
                            copied = used + place["project", PROJECTIONS - 1, 1] + 1
                        else:
                            copied = None
                        weigh(pair, k - 2, copied)
                    for n, (at_step, kind, arg, b) in enumerate(step_uses):
                        if at_step != k:
                            continue
                        owner = pair if k >= PHASE else pair - 1
                        if kind == "turn":
                            turn_attended(owner, used + n, b, arg)
                        elif kind == "out":
                            multiply_out(owner, used + n, arg)
                        else:
                            take_shared(used + n)
                            if arg == 0 and b == 0:
                                pe.wait_ge(w_lo_done, pair + 2)
                            project(arg, b)

            def finish():
                used = used_before(PAIRS - 1) + len(uses(False, True))
                pe.wait_ge(exp_done, PAIRS * STEPS)
                turn(PAIRS, -1)
                weigh(PAIRS, -2)
                weigh(PAIRS, -1)
                for c in range(CHUNKS):
                    turn_attended(PAIRS - 1, used + 2 * c, BATCH - 1, c)
                    multiply_out(PAIRS - 1, used + 2 * c + 1, c)

            loop(pe, body)
            finish()

        @block.vector
        def _(dve):
            def split_weights(pair):
                dve.wait_ge(w_in, (pair + 1) * 3 * 16)
                nc.vector.tensor_copy(w_hi[:], raw[:]).then_inc(w_hi_done, 1)
                dve.wait_ge(w_hi_done, pair + 1)
                nc.vector.tensor_tensor(w_lo[:], raw[:], w_hi[:].bitcast(F32), ALU.subtract).then_inc(w_lo_done, 1)

            def split_rotation(phase, r):
                n = phase * ROTATIONS + r
                dve.wait_ge(summed, n + 1)
                if isinstance(phase, int) and phase == 0:
                    if r > 1:
                        dve.wait_ge(q_in if r % 2 else k_in, r // 2 * 4 * 16)
                    nc.vector.tensor_copy(halves[r % 2][:, 0, :], rotated[r % 2][:]).then_inc(hi_done, 1)
                dve.wait_ge(hi_done, n + 1)
                nc.vector.tensor_tensor(halves[r % 2][:, 1, :], rotated[r % 2][:], halves[r % 2][:, 0, :].bitcast(F32),
                                        ALU.subtract).then_inc(lo_done, 1)

            def copy_turned(pair, k):
                at = k % SEQ_TILES
                kts = min(QUARTER, ORDER[at] + 1)
                dve.wait_ge(fill_done, fills_before(pair, k) + 1)
                nc.vector.tensor_copy(probsT[k % 2][:, 0:kts, :], turned[fill_at[at] % 2][:, 0:kts, :])\
                  .then_inc(low_copied, 1)

            def maximum(pair, k):
                n = (ORDER[k % SEQ_TILES] + 1) * P
                dve.wait_ge(scores_done, pair * STEPS + k + 1)
                block = scores[k % 2][:, n - P:n]
                nc.vector.tensor_tensor(block, block, mask[:], ALU.add).then_inc(masked, 1)
                dve.wait_ge(masked, pair * STEPS + k + 1)
                nc.vector.tensor_reduce(neg_max[:, k % RING:k % RING + 1], scores[k % 2][:, 0:n], AX.X, ALU.max,
                                        negate=True).then_inc(max_done, 1)

            def invert(pair, k):
                slot = slice(k % RING, k % RING + 1)
                dve.wait_ge(exp_done, pair * STEPS + k + 1)
                nc.vector.reciprocal(inverse[:, slot], sums[:, slot]).then_inc(inverse_done, 1)

            def divide(pair, k):
                unit, at = divmod(k % STEPS, SEQ_TILES)
                b, h = divmod(unit, 2)
                slot = slice(k % RING, k % RING + 1)
                dve.wait_ge(weighted_done, pair * STEPS + k + 1)
                dve.wait_ge(inverse_done, pair * STEPS + k + 1)
                nc.vector.tensor_scalar(attended[b][:, ORDER[at], h * HEAD_DIM:(h + 1) * HEAD_DIM], weighted[:],
                                        inverse[:, slot], None, ALU.mult).then_inc(attended_done, 1)

            def accumulate(n, b, c):
                dve.wait_ge(shared_done, n + 1)
                part = slice(b * SEQ + c * BANK, b * SEQ + (c + 1) * BANK)
                nc.vector.tensor_tensor(o1T[:, part], o1T[:, part], shared[:], ALU.add).then_inc(shared_free, 1)

            split_weights(0)
            dve.wait_ge(tables_in, 32)
            for r in range(ROTATIONS):
                part = slice(r // 2 * BANK, (r // 2 + 1) * BANK)
                dve.wait_ge(swapped_in[r % 2], (r // 2 + 1) * (P // HALF) * 16)
                nc.vector.tensor_tensor(by_sin[:], swapped[r % 2][:], sin[:, part], ALU.mult).then_inc(sin_done, 1)
                dve.wait_ge(cos_done, r + 1)
                dve.wait_ge(sin_done, r + 1)
                nc.vector.tensor_tensor(rotated[r % 2][:], rotated[r % 2][:], by_sin[:], ALU.add).then_inc(summed, 1)
                split_rotation(0, r)
            dve.wait_ge(cleared, 2)
            dve.wait_ge(masks, 1)
            maximum(0, 0)

            def body(pair, first, last):
                step_uses, place, used = uses(first, last), places(first, last), used_before(pair, first)
                for k in range(STEPS):
                    if k > 2 or not first:
                        divide(pair, k - 3)
                    if k + 1 < STEPS or not last:
                        maximum(pair, k + 1)
                    if k > 0 or not first:
                        invert(pair, k - 1)
                        copy_turned(pair, k - 1)
                    for n, (at_step, kind, arg, b) in enumerate(step_uses):
                        if at_step == k and kind == "out":
                            accumulate(used + n, b, arg)
                    ahead, at = divmod(k, PHASE)
                    if at in ROTATED_AT and not (last and ahead == BATCH - 1):
                        split_rotation(BATCH * pair + ahead + 1, ROTATED_AT[at])
                    if k == SPLIT_AT and not last:
                        dve.wait_ge(shared_done, used + place["project", PROJECTIONS - 1, 1] + 1)
                        split_weights(pair + 1)

            loop(dve, body)
            used = used_before(PAIRS - 1) + len(uses(False, True))
            divide(PAIRS, -3)
            copy_turned(PAIRS, -1)
            invert(PAIRS, -1)
            divide(PAIRS, -2)
            divide(PAIRS, -1)
            for c in range(CHUNKS):
                accumulate(used + 2 * c + 1, BATCH - 1, c)

        @block.scalar
        def _(act):
            def copy_projection(n, phase, r):
                act.wait_ge(shared_done, n + 1)
                if r > 1 or phase is not None:
                    count = (0 if phase is None else phase * ROTATIONS) + r - 1
                    act.wait_ge(cos_done, count)
                    act.wait_ge(sin_done, count)
                nc.scalar.activation(plain[r % 2][:], shared[:], ACT.Copy, scale=HEAD_DIM ** -0.5 if r % 2 else 1.0)\
                  .then_inc(shared_free, 1)

            def copy_values(n, j, b):
                act.wait_ge(shared_done, n + 1)
                tiles = slice((j - ROTATIONS) * QUARTER, (j - ROTATIONS + 1) * QUARTER)
                nc.scalar.activation(values[b][:, tiles, :], shared[:].rearrange("p (t d) -> p t d", d=P), ACT.Copy)\
                  .then_inc(shared_free, 1)

            def copy_attended(n, c):
                act.wait_ge(shared_done, n + 1)
                nc.scalar.activation(attendedT[c][:], shared[:], ACT.Copy).then_inc(shared_free, 1)

            def exponentials(pair, k):
                act.wait_ge(max_done, pair * STEPS + k + 1)
                wait_count(act, fill_done, fills_before(pair, k - RING + 1))
                n = (ORDER[k % SEQ_TILES] + 1) * P
                at = slice(k % RING, k % RING + 1)
                nc.scalar.activation(probs[k % RING][:, 0:n], scores[k % 2][:, 0:n], ACT.Exp, bias=neg_max[:, at],
                                     accum_out=sums[:, at]).then_inc(exp_done, 1)

            def copy_turned(pair, k):
                at = k % SEQ_TILES
                if fills_of[at] > 1:
                    kts = slice(QUARTER, ORDER[at] + 1)
                    act.wait_ge(fill_done, fills_before(pair, k) + 2)
                    nc.scalar.activation(probsT[k % 2][:, kts, :], turned[(fill_at[at] + 1) % 2][:, 0:ORDER[at] + 1 - QUARTER, :],
                                         ACT.Copy).then_inc(high_copied, 1)

            for j in range(PROJECTIONS):
                if j < ROTATIONS:
                    copy_projection(j, None, j)
                else:
                    copy_values(j, j, 0)
            exponentials(0, 0)

            def body(pair, first, last):
                step_uses, place, used = uses(first, last), places(first, last), used_before(pair, first)
                for k in range(STEPS):
                    if k > 0 or not first:
                        copy_turned(pair, k - 1)
                    if k + 1 < STEPS or not last:
                        exponentials(pair, k + 1)
                    for n, (at_step, kind, arg, b) in enumerate(step_uses):
                        if at_step != k:
                            continue
                        if kind == "turn":
                            copy_attended(used + n, arg)
                        elif kind == "project" and arg < ROTATIONS:
                            copy_projection(used + n, BATCH * pair + (1 if b else 2), arg)
                        elif kind == "project":
                            copy_values(used + n, arg, b)

            loop(act, body)
            used = used_before(PAIRS - 1) + len(uses(False, True))
            copy_turned(PAIRS, -1)
            for c in range(CHUNKS):
                copy_attended(used + 2 * c, c)


def project_out(nc, wo2, gammas, loaded, o1T, x, load_later, copy_later):
    QUARTER = BANK // P
    OWN = 3 * TILES // 4
    with ExitStack() as stack:
        m = Memory(nc, stack, "out_")
        stats = m.sb("stats", [P, TILES, 6])
        mean_var = m.sb("mean_var", [P, TILES, 2])
        var_eps = m.sb("var_eps", [P, TILES])
        root = m.sb("root", [P, TILES])
        rstd = m.sb("rstd", [P, TILES])
        shift = m.sb("shift", [P, TILES])
        scratch = m.sb("scratch", [P, TILES])
        y = m.sb("y", [P, TILES, DIM])
        product = [m.ps(f"product{c}", [P, BANK]) for c in range(ALL_CHUNKS)]
        chain, relu_done, product_done, var_ready, root_ready, shift_ready, other_ready, pool_chain = (
            m.sem(n) for n in ("chain", "relu_done", "product_done", "var_ready", "root_ready", "shift_ready",
                               "other_ready", "pool_chain"))
        block = stack.enter_context(nc.Block())

        def tile(t):
            c, i = divmod(t, QUARTER)
            return product[c][:, i * P:(i + 1) * P]

        @block.sync
        def _(sync):
            load_later(sync)

        def gamma_of(tiles):
            return gammas[:].rearrange("p (a n) -> p a n", a=1).broadcast_to([P, tiles, DIM])

        @block.tensor
        def _(pe):
            pe.wait_ge(loaded, 32)
            for t in range(TILES):
                c, i = divmod(t, QUARTER)
                pe.wait_ge(relu_done, c + 1)
                last = nc.tensor.matmul(tile(t), o1T[:, t * P:(t + 1) * P], wo2[:], start=True, stop=True)
                if i == QUARTER - 1:
                    last.then_inc(product_done, 1)

        @block.scalar
        def _(act):
            act.wait_ge(var_ready, 1)
            nc.scalar.activation(root[:], var_eps[:], ACT.Sqrt).then_inc(root_ready, 1)
            act.wait_ge(shift_ready, 1)
            for t in range(OWN, TILES):
                last = nc.scalar.activation(y[:, t, :], tile(t), ACT.Identity, bias=shift[:, t:t + 1], scale=rstd[:, t:t + 1])
            last.then_inc(other_ready, 1)
            copy_later(act)

        @block.gpsimd
        def _(pool):
            link = counter(pool, pool_chain)
            pool.wait_ge(loaded, 32)
            pool.wait_ge(other_ready, 1)
            link(nc.gpsimd.tensor_tensor(y[:, OWN:, :], y[:, OWN:, :], gamma_of(TILES - OWN), ALU.mult))
            link(nc.gpsimd.tensor_tensor(x[:, OWN:, :], x[:, OWN:, :], y[:, OWN:, :], ALU.add))

        @block.vector
        def _(dve):
            link = counter(dve, chain)
            for c in range(ALL_CHUNKS):
                part = o1T[:, c * BANK:(c + 1) * BANK]
                nc.vector.tensor_scalar(part, part, 0.0, None, ALU.max).then_inc(relu_done, 1)
            for t in range(TILES):
                if t % QUARTER == 0:
                    dve.wait_ge(product_done, t // QUARTER + 1)
                last = nc.vector.bn_stats(stats[:, t, :], tile(t))
            link(last)
            for t in range(TILES):
                last = nc.vector.bn_aggr(mean_var[:, t, :], stats[:, t, :])
            link(last)
            reciprocal_deviation(nc, dve, link, mean_var, var_eps, var_ready, root, root_ready, rstd, scratch)
            nc.vector.scalar_tensor_tensor(shift[:], mean_var[:, :, 0], -1.0, rstd[:], ALU.mult, ALU.mult)\
              .then_inc(shift_ready, 1)
            for t in range(OWN):
                last = nc.vector.tensor_scalar(y[:, t, :], tile(t), mean_var[:, t, 0:1], rstd[:, t:t + 1],
                                               ALU.subtract, ALU.mult)
            link(last)
            dve.wait_ge(loaded, 32)
            link(nc.vector.tensor_tensor(y[:, 0:OWN, :], y[:, 0:OWN, :], gamma_of(OWN), ALU.mult))
            link(nc.vector.tensor_tensor(x[:, 0:OWN, :], x[:, 0:OWN, :], y[:, 0:OWN, :], ALU.add))


def feed_forward(nc, gates_dram, gate, w1_hi, w1_lo, w2_hi, w2_lo, xT_hi, xT_lo, sumT, name, nth):
    LAG, RING = 3, 4
    with ExitStack() as stack:
        m = Memory(nc, stack, name)
        gates = m.sb("gates", [P, EXPERTS, BANK])
        hidden = [m.sb(f"hidden{i}", [P, BANK]) for i in range(RING)]
        hidden_hi = [m.sb(f"hidden_hi{i}", [P, BANK], F32R) for i in range(RING)]
        hidden_lo = [m.sb(f"hidden_lo{i}", [P, BANK], F32R) for i in range(RING)]
        gated = [m.sb(f"gated{i}", [P, BANK]) for i in range(2)]
        up_ps = [m.ps(f"up{i}", [P, BANK]) for i in range(RING)]
        down_ps = [m.ps(f"down{i}", [P, BANK]) for i in range(2)]
        gates_in = [m.sem(f"gates_in{e}") for e in range(EXPERTS)]
        up_done, hi_done, relu_done, lo_done, down_done, gated_done, summed = (
            m.sem(n) for n in ("up_done", "hi_done", "relu_done", "lo_done", "down_done", "gated_done", "summed"))
        block = stack.enter_context(nc.Block())

        @block.sync
        def _(sync):
            def load_gates(chunk, e):
                rows = gates_dram[e:e + 1, bass.ds(chunk * BANK, BANK)].broadcast_to([P, BANK])
                sync.dma_start(gates[:, e, :], rows).then_inc(gates_in[e], 16)

            sync.wait_ge(gate.stored, 16 * nth)
            for e in range(EXPERTS):
                load_gates(0, e)
            with sync.Fori(0, ALL_CHUNKS - 1) as chunk:
                for e in range(EXPERTS):
                    sync.wait_ge(gated_done, chunk * EXPERTS + e + 1)
                    load_gates(chunk + 1, e)

        @block.tensor
        def _(pe):
            with pe.Fori(0, ALL_CHUNKS) as chunk:
                tokens = bass.ds(chunk * BANK, BANK)
                before = chunk * ALL_SLICES

                def up(n):
                    if n >= RING:
                        pe.wait_ge(relu_done, before + n - RING + 1)
                    w = slice(n * P, (n + 1) * P)
                    for i, (wt, xt) in enumerate(((w1_hi, xT_hi), (w1_hi, xT_lo), (w1_lo, xT_hi))):
                        last = nc.tensor.matmul(up_ps[n % RING][:], wt[:, w], xt[:, tokens], start=i == 0, stop=i == 2)
                    last.then_inc(up_done, 1)

                def down(n):
                    e, s = divmod(n, SLICES)
                    w = slice(n * P, (n + 1) * P)
                    pe.wait_ge(lo_done, before + n + 1)
                    if s == 0 and e >= 2:
                        pe.wait_ge(gated_done, chunk * EXPERTS + e - 1)
                    for i, (wt, ht) in enumerate(((w2_hi, hidden_hi), (w2_hi, hidden_lo), (w2_lo, hidden_hi))):
                        last = nc.tensor.matmul(down_ps[e % 2][:], wt[:, w], ht[n % RING][:],
                                                start=s == 0 and i == 0, stop=s == SLICES - 1 and i == 2)
                    last.then_inc(down_done, 1)

                for n in range(LAG):
                    up(n)
                for n in range(ALL_SLICES):
                    if n + LAG < ALL_SLICES:
                        up(n + LAG)
                    down(n)

        @block.scalar
        def _(act):
            with act.Fori(0, ALL_CHUNKS) as chunk:
                before = chunk * ALL_SLICES
                for n in range(ALL_SLICES):
                    act.wait_ge(up_done, before + n + 1)
                    if n >= RING:
                        act.wait_ge(down_done, before + n - RING + 1)
                    bias = gate.b1T[:, n:n + 1]
                    nc.scalar.activation(hidden_hi[n % RING][:], up_ps[n % RING][:], ACT.Relu, bias=bias)\
                      .then_inc(hi_done, 1)
                    nc.scalar.activation(hidden[n % RING][:], up_ps[n % RING][:], ACT.Relu, bias=bias)\
                      .then_inc(relu_done, 1)

        @block.vector
        def _(dve):
            with dve.Fori(0, ALL_CHUNKS) as chunk:
                before = chunk * ALL_SLICES
                tokens = bass.ds(chunk * BANK, BANK)

                def combine(e):
                    dve.wait_ge(gates_in[e], (chunk + 1) * 16)
                    dve.wait_ge(down_done, before + (e + 1) * SLICES)
                    to = gated[e % 2][:] if e else sumT[:, tokens]
                    nc.vector.scalar_tensor_tensor(to, down_ps[e % 2][:], gate.b2T[:, e:e + 1], gates[:, e, :],
                                                   ALU.add, ALU.mult).then_inc(gated_done, 1)
                    dve.wait_ge(gated_done, chunk * EXPERTS + e + 1)
                    if e:
                        nc.vector.tensor_tensor(sumT[:, tokens], sumT[:, tokens], gated[e % 2][:], ALU.add)\
                          .then_inc(summed, 1)
                        dve.wait_ge(summed, chunk * (EXPERTS - 1) + e)

                for n in range(ALL_SLICES):
                    dve.wait_ge(hi_done, before + n + 1)
                    dve.wait_ge(relu_done, before + n + 1)
                    nc.vector.tensor_tensor(hidden_lo[n % RING][:], hidden[n % RING][:],
                                            hidden_hi[n % RING][:].bitcast(F32), ALU.subtract).then_inc(lo_done, 1)
                    if n >= 2 * SLICES - 1 and n % SLICES == SLICES - 1:
                        combine(n // SLICES - 1)
                combine(EXPERTS - 1)


def add_turned(nc, sumT, x, ident, name, out=None):
    with ExitStack() as stack:
        m = Memory(nc, stack, name)
        turned = [m.ps(f"turned{i}", [P, BANK]) for i in range(ALL_CHUNKS)]
        turn_done, added, stored = m.sem("turn_done"), m.sem("added"), m.sem("stored")
        block = stack.enter_context(nc.Block())
        per = BANK // P

        @block.tensor
        def _(pe):
            for t in range(TILES):
                c, i = divmod(t, per)
                last = nc.tensor.transpose(turned[c][:, i * P:(i + 1) * P], sumT[:, t * P:(t + 1) * P], ident[:])
                if i == per - 1:
                    last.then_inc(turn_done, 1)

        @block.vector
        def _(dve):
            for c in range(ALL_CHUNKS):
                dve.wait_ge(turn_done, c + 1)
                part = x[:, c * per:(c + 1) * per, :]
                nc.vector.tensor_tensor(part, part, turned[c][:].rearrange("p (t d) -> p t d", d=DIM), ALU.add)\
                  .then_inc(added, 1)

        if out is not None:
            @block.sync
            def _(sync):
                for c in range(ALL_CHUNKS):
                    sync.wait_ge(added, c + 1)
                    sync.dma_start(out[:, c * per:(c + 1) * per, :], x[:, c * per:(c + 1) * per, :]).then_inc(stored, 16)
                sync.wait_ge(stored, 16 * ALL_CHUNKS)


def full_attention(nc, qk_hi, qk_lo, vo_sb, xn, xT_hi, xT_lo, ident, x, probsT):
    QUARTER = BANK // P
    FILLS = SEQ_TILES // QUARTER
    PIECE = 2
    Y_AT = {2: 2, 4: 3}
    with ExitStack() as stack:
        m = Memory(nc, stack, "full_")
        yT = m.sb("yT", [P, TOKENS])
        yT_hi = m.sb("yT_hi", [P, TOKENS], F32R)
        yT_lo = m.sb("yT_lo", [P, TOKENS], F32R)
        neg_max = m.sb("neg_max", [P, TILES])
        sums = m.sb("sums", [P, TILES])
        inverse = m.sb("inverse", [P, TILES])
        probs = [m.sb(f"probs{i}", [P, SEQ]) for i in range(2)]
        meanT = [m.sb(f"meanT{i}", [P, BANK]) for i in range(2)]
        scores = [m.ps(f"scores{i}", [P, SEQ]) for i in range(2)]
        turned = [m.ps(f"turned{i}", [P, QUARTER, P]) for i in range(2)]
        weighted = m.ps("weighted", [P, BANK])
        result = m.ps("result", [P, QUARTER, DIM])
        y_ps = [result[:].rearrange("p t d -> p (t d)"), weighted[:]] + [result[:].rearrange("p t d -> p (t d)")] * 2
        (y_done, y_copied, y_hi_done, y_lo_done, scores_done, max_done, exp_done,
         inverse_done, fill_done, fill_copied, weighted_done, mean_done, result_done, result_read) = (
            m.sem(n) for n in ("y_done", "y_copied", "y_hi_done", "y_lo_done",
                               "scores_done", "max_done", "exp_done", "inverse_done", "fill_done", "fill_copied",
                               "weighted_done", "mean_done", "result_done", "result_read"))
        block = stack.enter_context(nc.Block())

        @block.tensor
        def _(pe):
            def multiply_qk(c):
                part = slice(c * BANK, (c + 1) * BANK)
                if c >= 2:
                    pe.wait_ge(y_copied, c)
                for i, (wt, xt) in enumerate(((qk_hi, xT_hi), (qk_hi, xT_lo), (qk_lo, xT_hi))):
                    last = nc.tensor.matmul(y_ps[c], wt[:], xt[:, part], start=i == 0, stop=i == 2)
                last.then_inc(y_done, 1)

            def score(k):
                b = k // SEQ_TILES
                cols = slice(k * P, (k + 1) * P)
                pe.wait_ge(y_lo_done, k // QUARTER + 1)
                if k >= 2:
                    pe.wait_ge(exp_done, k - 1)
                for c in range(CHUNKS):
                    keys = slice(b * SEQ + c * BANK, b * SEQ + (c + 1) * BANK)
                    for i, (yt, xt) in enumerate(((yT_hi, xT_hi), (yT_hi, xT_lo), (yT_lo, xT_hi))):
                        last = nc.tensor.matmul(scores[k % 2][:, c * BANK:(c + 1) * BANK], yt[:, cols], xt[:, keys],
                                                start=i == 0, stop=i == 2)
                last.then_inc(scores_done, 1)

            def turn(k):
                pe.wait_ge(exp_done, k + 1)
                for g in range(FILLS):
                    fill = k * FILLS + g
                    if fill >= 2:
                        pe.wait_ge(fill_copied, fill - 1)
                    for i in range(QUARTER):
                        kt = g * QUARTER + i
                        last = nc.tensor.transpose(turned[fill % 2][:, i, :], probs[k % 2][:, kt * P:(kt + 1) * P], ident[:])
                    last.then_inc(fill_done, 1)

            def weigh(j, piece):
                b = j // CHUNKS
                if piece == 0:
                    pe.wait_ge(fill_copied, (j + 1) * QUARTER * FILLS)
                    if j >= 1:
                        pe.wait_ge(mean_done, j)
                    else:
                        pe.wait_ge(y_copied, 2)
                for kt in range(piece * PIECE, (piece + 1) * PIECE):
                    last = nc.tensor.matmul(weighted[:], xn[:, b * SEQ_TILES + kt, :], probsT[j % 2][:, kt, :],
                                            start=kt == 0, stop=kt == SEQ_TILES - 1)
                if piece == SEQ_TILES // PIECE - 1:
                    last.then_inc(weighted_done, 1)

            def multiply_out(j):
                pe.wait_ge(mean_done, j + 1)
                if j >= 1:
                    pe.wait_ge(result_read, j)
                else:
                    pe.wait_ge(y_copied, ALL_CHUNKS)
                for i in range(QUARTER):
                    last = nc.tensor.matmul(result[:, i, :], meanT[j % 2][:, i * P:(i + 1) * P], vo_sb[:],
                                            start=True, stop=True)
                last.then_inc(result_done, 1)

            multiply_qk(0)
            score(0)
            multiply_qk(1)
            for k in range(TILES + 2 * QUARTER):
                if k + 1 < TILES:
                    score(k + 1)
                if k in Y_AT:
                    multiply_qk(Y_AT[k])
                if 1 <= k <= TILES:
                    turn(k - 1)
                j, piece = divmod(k - QUARTER - 1, QUARTER)
                if 0 <= j < ALL_CHUNKS:
                    weigh(j, piece)
                if piece == 1 and 0 <= j - 1 < ALL_CHUNKS:
                    multiply_out(j - 1)

        @block.vector
        def _(dve):
            def split_y(c):
                part = slice(c * BANK, (c + 1) * BANK)
                dve.wait_ge(y_copied, c + 1)
                nc.vector.tensor_copy(yT_hi[:, part], yT[:, part]).then_inc(y_hi_done, 1)
                dve.wait_ge(y_hi_done, c + 1)
                nc.vector.tensor_tensor(yT_lo[:, part], yT[:, part], yT_hi[:, part].bitcast(F32),
                                        ALU.subtract).then_inc(y_lo_done, 1)

            def add_result(j):
                dve.wait_ge(result_done, j + 1)
                for i in range(QUARTER):
                    t = j * QUARTER + i
                    last = nc.vector.scalar_tensor_tensor(x[:, t, :], result[:, i, :], inverse[:, t:t + 1], x[:, t, :],
                                                          ALU.mult, ALU.add)
                last.then_inc(result_read, 1)

            split_y(0)
            for k in range(TILES + 2 * QUARTER):
                if k < TILES:
                    dve.wait_ge(scores_done, k + 1)
                    nc.vector.tensor_reduce(neg_max[:, k:k + 1], scores[k % 2][:], AX.X, ALU.max,
                                            negate=True).then_inc(max_done, 1)
                if k == 0:
                    split_y(1)
                if k - 1 in Y_AT:
                    split_y(Y_AT[k - 1])
                if 1 <= k <= TILES:
                    dve.wait_ge(exp_done, k)
                    nc.vector.reciprocal(inverse[:, k - 1:k], sums[:, k - 1:k]).then_inc(inverse_done, 1)
                j, piece = divmod(k - QUARTER - 1, QUARTER)
                if piece == 1 and 0 <= j - 1 < ALL_CHUNKS:
                    dve.wait_ge(inverse_done, j * QUARTER)
                    add_result(j - 1)

        @block.scalar
        def _(act):
            def copy_y(c):
                act.wait_ge(y_done, c + 1)
                nc.scalar.activation(yT[:, c * BANK:(c + 1) * BANK], y_ps[c], ACT.Copy, scale=float(DIM) ** -0.5)\
                  .then_inc(y_copied, 1)

            copy_y(0)
            copy_y(1)
            for k in range(TILES + 2 * QUARTER):
                if k < TILES:
                    act.wait_ge(max_done, k + 1)
                    nc.scalar.activation(probs[k % 2][:], scores[k % 2][:], ACT.Exp, bias=neg_max[:, k:k + 1],
                                         accum_out=sums[:, k:k + 1]).then_inc(exp_done, 1)
                if k in Y_AT:
                    copy_y(Y_AT[k])
                if 1 <= k <= TILES:
                    j, t = divmod(k - 1, QUARTER)
                    if t == 0 and j >= 2:
                        act.wait_ge(weighted_done, j - 1)
                    for g in range(FILLS):
                        fill = (k - 1) * FILLS + g
                        act.wait_ge(fill_done, fill + 1)
                        nc.scalar.activation(probsT[j % 2][:, g * QUARTER:(g + 1) * QUARTER, t * P:(t + 1) * P],
                                             turned[fill % 2][:], ACT.Copy).then_inc(fill_copied, 1)
                j, piece = divmod(k - QUARTER - 1, QUARTER)
                if piece == QUARTER - 1 and 0 <= j < ALL_CHUNKS:
                    act.wait_ge(weighted_done, j + 1)
                    nc.scalar.activation(meanT[j % 2][:], weighted[:], ACT.Copy).then_inc(mean_done, 1)


def hybrid_layer(nc, x_dram, w_qkv, w_o1, w_o2, gamma, qk, vo, wg, bg, w1, b1, w2, b2, cos_table, sin_table, out):
    x_rows = x_dram.rearrange("b (t p) d -> p (b t) d", p=P)
    out_rows = out.rearrange("b (t p) d -> p (b t) d", p=P)
    gates_dram = nc.dram_tensor("gates", (EXPERTS, TOKENS), F32, kind="Internal").ap()
    with ExitStack() as stack:
        m = Memory(nc, stack)
        ident = m.sb("ident", [P, P])
        x = m.sb("x", [P, TILES, DIM])
        xT_hi = m.sb("xT_hi", [P, TOKENS], F32R)
        xT_lo = m.sb("xT_lo", [P, TOKENS], F32R)
        sumT = m.sb("sumT", [P, TOKENS])
        ident_done = m.sem("ident_done")

        with nc.Block() as block:
            @block.gpsimd
            def _(pool):
                nc.gpsimd.memset(ident[:], 0.0).then_inc(ident_done, 1)
                pool.wait_ge(ident_done, 1)
                nc.gpsimd.affine_select(out=ident[:], in_=ident[:], compare_op=ALU.not_equal, fill=1.0, base=0,
                                        pattern=[[-1, P]], channel_multiplier=1)

        gate = GateInputs(m)
        wo2 = m.sb("wo2", [P, DIM])
        gammas = m.sb("gammas", [P, DIM])
        out_inputs_loaded, qk_loaded, qk_hi_done = m.sem("out_inputs_loaded"), m.sem("qk_loaded"), m.sem("qk_hi_done")
        weights_loaded, hi_split = m.sem("expert_weights_loaded"), m.sem("hi_split")

        def load_all(sync, loaded):
            per = BANK // P
            for c in range(ALL_CHUNKS):
                sync.dma_start(x[:, c * per:(c + 1) * per, :], x_rows[:, c * per:(c + 1) * per, :]).then_inc(loaded[c], 16)
            load_weights(sync, 0)
            sync.dma_start(cos[:], cos_table).then_inc(tables_in, 16)
            sync.dma_start(sin[:], sin_table).then_inc(tables_in, 16)
            gate.load(sync, wg, bg, b1, b2)
            sync.dma_start(wo2[:], w_o2).then_inc(out_inputs_loaded, 16)
            sync.dma_start(gammas[:], gamma.rearrange("(a n) -> a n", a=1).broadcast_to([P, DIM])).then_inc(out_inputs_loaded, 16)

        tables_in, w_in = m.sem("tables_in"), m.sem("w_in")
        raw = m.sb("w_raw", [P, 3, P])
        cos = m.sb("cos", [P, SEQ])
        sin = m.sb("sin", [P, SEQ])

        def load_weights(sync, pair):
            for j in range(3):
                sync.dma_start(raw[:, j, :], w_qkv[:, bass.ds(pair * P + j * INNER, P)]).then_inc(w_in, 16)

        with ExitStack() as early:
            e = Memory(nc, early, "early_")
            normalise_and_transpose(nc, x, e.sb("xn", [P, TILES, DIM]), e.sb("xT", [P, TOKENS]), xT_hi, xT_lo, ident,
                                    "ln1_", load_all)
        raw1 = m.sb("raw_w1", [P, EXPERTS, HIDDEN])
        w1_hi = m.sb("w1_hi", [P, EXPERTS * HIDDEN], F32R)
        w1_lo = m.sb("w1_lo", [P, EXPERTS * HIDDEN], F32R)

        def load_up(sync):
            sync.dma_start(raw1[:], w1.rearrange("e d h -> d e h")).then_inc(weights_loaded, 16)

        def load_down(sync):
            sync.dma_start(qk_raw[:], qk).then_inc(qk_loaded, 16)
            sync.dma_start(vo_sb[:], vo).then_inc(qk_loaded, 16)
            sync.dma_start(raw2[:], w2.rearrange("e (s h) d -> h (e s) d", h=P)).then_inc(weights_loaded, 16)

        def splitter(raw, hi, lo, n):
            flat = raw[:].rearrange("p a b -> p (a b)")

            def split(pool, copy=True):
                pool.wait_ge(weights_loaded, 16 * (n + 1))
                for e in range(EXPERTS):
                    cols = slice(e * HIDDEN, (e + 1) * HIDDEN)
                    if copy:
                        nc.gpsimd.tensor_copy(hi[:, cols], flat[:, cols]).then_inc(hi_split, 1)
                    pool.wait_ge(hi_split, n * EXPERTS + e + 1)
                    nc.gpsimd.tensor_tensor(lo[:, cols], flat[:, cols], hi[:, cols].bitcast(F32), ALU.subtract)
            return split

        causal_attention(nc, w_qkv, w_o1, cos, sin, tables_in, raw, w_in, load_weights, xT_hi, xT_lo, ident, sumT, load_up,
                         splitter(raw1, w1_hi, w1_lo, 0))
        qk_raw = m.sb("qk_raw", [P, DIM])
        qk_hi = m.sb("qk_hi", [P, DIM], F32R)
        qk_lo = m.sb("qk_lo", [P, DIM], F32R)
        vo_sb = m.sb("vo", [P, DIM])
        raw2 = m.sb("raw_w2", [P, ALL_SLICES, DIM])
        w2_hi = m.sb("w2_hi", [P, ALL_SLICES * DIM], F32R)
        w2_lo = m.sb("w2_lo", [P, ALL_SLICES * DIM], F32R)
        xn = m.sb("xn", [P, TILES, DIM])
        xT = m.sb("xT", [P, TOKENS])

        def copy_down(experts):
            def copy(act):
                act.wait_ge(weights_loaded, 32)
                for e in experts:
                    cols = slice(e * HIDDEN, (e + 1) * HIDDEN)
                    nc.scalar.activation(w2_hi[:, cols], raw2[:].rearrange("p a b -> p (a b)")[:, cols], ACT.Copy)\
                      .then_inc(hi_split, 1)
            return copy

        project_out(nc, wo2, gammas, out_inputs_loaded, sumT, x, load_down, copy_down(range(EXPERTS // 2)))
        normalise_and_transpose(nc, x, xn, xT, xT_hi, xT_lo, ident, "ln2_", gate=gate, gates_dram=gates_dram,
                                split=lambda pool: splitter(raw2, w2_hi, w2_lo, 1)(pool, copy=False),
                                copy=copy_down(range(EXPERTS // 2, EXPERTS)))
        feed_forward(nc, gates_dram, gate, w1_hi, w1_lo, w2_hi, w2_lo, xT_hi, xT_lo, sumT, "ff1_", 1)

        def split_qk(pool):
            pool.wait_ge(qk_loaded, 32)
            nc.gpsimd.tensor_copy(qk_hi[:], qk_raw[:]).then_inc(qk_hi_done, 1)
            pool.wait_ge(qk_hi_done, 1)
            nc.gpsimd.tensor_tensor(qk_lo[:], qk_raw[:], qk_hi[:].bitcast(F32), ALU.subtract)

        normalise_and_transpose(nc, x, xn, xT, xT_hi, xT_lo, ident, "ln3_", addT=sumT, split=split_qk)
        probsT = [raw1[:], raw2[:].rearrange("p (k s) d -> p k (s d)", s=SLICES)]
        full_attention(nc, qk_hi, qk_lo, vo_sb, xn, xT_hi, xT_lo, ident, x, probsT)
        normalise_and_transpose(nc, x, xn, xT, xT_hi, xT_lo, ident, "ln4_", gate=gate, gates_dram=gates_dram)
        feed_forward(nc, gates_dram, gate, w1_hi, w1_lo, w2_hi, w2_lo, xT_hi, xT_lo, sumT, "ff2_", 2)
        add_turned(nc, sumT, x, ident, "add_", out_rows)


_INS = ['L0_attn_a_x', 'L0_attn_a_W_qkv', 'L0_attn_a_W_o1', 'L0_attn_a_W_o2', 'L0_attn_a_gamma', 'L0_attn_b_QK',
        'L0_attn_b_VO', 'L0_ffn_Wg', 'L0_ffn_bg', 'L0_ffn_W1', 'L0_ffn_b1', 'L0_ffn_W2', 'L0_ffn_b2']


def rotation_tables():
    inv_freq = (np.float32(1.0) / np.power(np.float32(10000.0),
                np.arange(0, HEAD_DIM, 2, dtype=np.float32) / np.float32(HEAD_DIM))).astype(np.float32)
    angle = inv_freq[:, None] * np.arange(SEQ, dtype=np.float32)[None, :]
    cos, sin = np.cos(angle), np.sin(angle)
    return np.concatenate([cos] * 4, 0), np.concatenate([-sin, sin] * 2, 0)


def kernel(**inputs):
    import concourse.bacc as bacc
    from concourse.bass_utils import run_bass_kernel_spmd

    nc = bacc.Bacc("TRN2", target_bir_lowering=False, num_devices=1)
    arrays, args = {}, []
    cos, sin = rotation_tables()
    for name, a in [(n, inputs[n]) for n in _INS] + [("cos_table", cos), ("sin_table", sin)]:
        a = np.ascontiguousarray(a)
        arrays[f"in_{name}"] = a
        args.append(nc.dram_tensor(f"in_{name}", a.shape, mybir.dt.from_np(a.dtype), kind="ExternalInput").ap())
    out = nc.dram_tensor("out_0", (BATCH, SEQ, DIM), F32, kind="ExternalOutput").ap()
    hybrid_layer(nc, *args, out)
    r = run_bass_kernel_spmd(nc, [arrays], core_ids=[0])
    return r.results[0]["out_0"]
```
